# Optimizing a Trainium2 kernel written in Bass

```python
import numpy as np
import jax
import jax.numpy as jnp

def _softmax(x, axis=-1):
    return jax.nn.softmax(x, axis=axis)

def _gelu(x):
    return jax.nn.gelu(x, approximate=True)

def _silu(x):
    return jax.nn.silu(x)

def _sigmoid(x):
    return jax.nn.sigmoid(x)

def _layernorm(x, axis=-1, eps=1e-05):
    m = jnp.mean(x, axis=axis, keepdims=True)
    v = jnp.var(x, axis=axis, keepdims=True)
    return (x - m) / jnp.sqrt(v + eps)

def _scatter_add(tgt, idx, src, axis=0):
    return tgt.at[idx].add(src)

def _segment_sum(src, seg, n):
    return jax.ops.segment_sum(src, seg, n)
kernel_name = 'mk_hybrid_d1_jaxref_r8_d63920'

def setup_inputs(seed: int=0):
    np.random.seed(seed)
    _w = jnp.asarray

    def _L0_attn_a_setup():
        import jax, jax.numpy as jnp
        import numpy as np
        B, T, HID = (2, 256, 256)
        H, DK, DV = (16, 128, 128)
        KC = 4
        EPS = 1e-06

        def short_conv(x, w):
            Tn = x.shape[1]
            xp = jnp.pad(x, ((0, 0), (KC - 1, 0), (0, 0)))
            out = xp[:, 0:Tn, :] * w[:, 0]
            for i in range(1, KC):
                out = out + xp[:, i:i + Tn, :] * w[:, i]
            return jax.nn.silu(out)

        def _l2norm(x):
            x = x.astype(jnp.float32)
            return x * jax.lax.rsqrt(jnp.sum(x * x, -1, keepdims=True) + 1e-06)
        key = jax.random.key(seed)
        ks = jax.random.split(key, 16)
        s = 0.02
        mk = lambda k, shp, sc=s: jax.random.normal(k, shp, jnp.float32) * sc
        a_init = jax.random.uniform(ks[7], (H,), minval=1.0, maxval=16.0, dtype=jnp.float32)
        return {'hidden_states': jax.random.normal(ks[0], (B, T, HID), jnp.float32), 'Wq': mk(ks[1], (HID, H * DK)), 'Wk': mk(ks[2], (HID, H * DK)), 'Wv': mk(ks[3], (HID, H * DV)), 'conv_q': mk(ks[4], (H * DK, KC), 0.3), 'conv_k': mk(ks[5], (H * DK, KC), 0.3), 'conv_v': mk(ks[6], (H * DV, KC), 0.3), 'A_log': jnp.log(a_init).reshape(1, 1, H, 1), 'Wfa': mk(ks[8], (HID, DV)), 'Wfb': mk(ks[9], (DV, H * DV)), 'dt_bias': jnp.zeros((H * DV,), jnp.float32), 'Wb': mk(ks[10], (HID, H)), 'Wga': mk(ks[11], (HID, DV)), 'Wgb': mk(ks[12], (DV, H * DV)), 'norm_w': jnp.ones((DV,), jnp.float32), 'Wo': mk(ks[13], (H * DV, HID))}
    _L0_attn_a_in = _L0_attn_a_setup()

    def _L0_attn_b_setup():
        import jax, jax.numpy as jnp
        import numpy as np
        D_MODEL = 256
        STATE = 16
        KCONV = 4
        EXPAND = 2
        D_INNER = D_MODEL * EXPAND
        EPS = 1e-05

        def _silu(v):
            return v * jax.nn.sigmoid(v)
        key = jax.random.key(seed)
        ks = jax.random.split(key, 10)
        s = 0.02
        x = jax.random.normal(ks[0], (2, 256, D_MODEL), dtype=jnp.float32)
        norm_w = jnp.ones((D_MODEL,), jnp.float32)
        in_proj_w = jax.random.normal(ks[1], (D_INNER * 2, D_MODEL), jnp.float32) * s
        conv_w = jax.random.normal(ks[2], (D_INNER, 1, KCONV), jnp.float32) * s
        conv_b = jnp.zeros((D_INNER,), jnp.float32)
        x_proj_w = jax.random.normal(ks[3], (STATE * 2 + 1, D_INNER), jnp.float32) * s
        dt_w = jax.random.normal(ks[4], (D_INNER, 1), jnp.float32) * s
        dt_b = jnp.zeros((D_INNER,), jnp.float32)
        A_log = jnp.log(jnp.broadcast_to(jnp.arange(1, STATE + 1, dtype=jnp.float32)[None, :], (D_INNER, STATE)))
        D_param = jnp.ones((D_INNER,), jnp.float32)
        out_proj_w = jax.random.normal(ks[5], (D_MODEL, D_INNER), jnp.float32) * s
        return {'x': x, 'norm_w': norm_w, 'in_proj_w': in_proj_w, 'conv_w': conv_w, 'conv_b': conv_b, 'x_proj_w': x_proj_w, 'dt_w': dt_w, 'dt_b': dt_b, 'A_log': A_log, 'D_param': D_param, 'out_proj_w': out_proj_w}
    _L0_attn_b_in = _L0_attn_b_setup()

    def _L0_ffn_setup():
        import jax, jax.numpy as jnp
        import numpy as np
        DIM_IN = 256
        DIM_HIDDEN = 1024
        key = jax.random.key(seed)
        k_x, k_g, k_u, k_d = jax.random.split(key, 4)
        s_in = 1.0 / np.sqrt(DIM_IN)
        s_hid = 1.0 / np.sqrt(DIM_HIDDEN)
        x = jax.random.normal(k_x, (4, 256, DIM_IN), dtype=jnp.float32)
        w_gate = jax.random.uniform(k_g, (DIM_HIDDEN, DIM_IN), jnp.float32, -s_in, s_in)
        w_up = jax.random.uniform(k_u, (DIM_HIDDEN, DIM_IN), jnp.float32, -s_in, s_in)
        w_down = jax.random.uniform(k_d, (DIM_IN, DIM_HIDDEN), jnp.float32, -s_hid, s_hid)
        return {'x': x, 'w_gate': w_gate, 'w_up': w_up, 'w_down': w_down}
    _L0_ffn_in = _L0_ffn_setup()
    _d = {'L0_attn_a_hidden_states': _L0_attn_a_in['hidden_states'], 'L0_attn_a_Wq': _L0_attn_a_in['Wq'], 'L0_attn_a_Wk': _L0_attn_a_in['Wk'], 'L0_attn_a_Wv': _L0_attn_a_in['Wv'], 'L0_attn_a_conv_q': _L0_attn_a_in['conv_q'], 'L0_attn_a_conv_k': _L0_attn_a_in['conv_k'], 'L0_attn_a_conv_v': _L0_attn_a_in['conv_v'], 'L0_attn_a_A_log': _L0_attn_a_in['A_log'], 'L0_attn_a_Wfa': _L0_attn_a_in['Wfa'], 'L0_attn_a_Wfb': _L0_attn_a_in['Wfb'], 'L0_attn_a_dt_bias': _L0_attn_a_in['dt_bias'], 'L0_attn_a_Wb': _L0_attn_a_in['Wb'], 'L0_attn_a_Wga': _L0_attn_a_in['Wga'], 'L0_attn_a_Wgb': _L0_attn_a_in['Wgb'], 'L0_attn_a_norm_w': _L0_attn_a_in['norm_w'], 'L0_attn_a_Wo': _L0_attn_a_in['Wo'], 'L0_attn_b_norm_w': _L0_attn_b_in['norm_w'], 'L0_attn_b_in_proj_w': _L0_attn_b_in['in_proj_w'], 'L0_attn_b_conv_w': _L0_attn_b_in['conv_w'], 'L0_attn_b_conv_b': _L0_attn_b_in['conv_b'], 'L0_attn_b_x_proj_w': _L0_attn_b_in['x_proj_w'], 'L0_attn_b_dt_w': _L0_attn_b_in['dt_w'], 'L0_attn_b_dt_b': _L0_attn_b_in['dt_b'], 'L0_attn_b_A_log': _L0_attn_b_in['A_log'], 'L0_attn_b_D_param': _L0_attn_b_in['D_param'], 'L0_attn_b_out_proj_w': _L0_attn_b_in['out_proj_w'], 'L0_ffn_w_gate': _L0_ffn_in['w_gate'], 'L0_ffn_w_up': _L0_ffn_in['w_up'], 'L0_ffn_w_down': _L0_ffn_in['w_down']}
    _x0 = _d['L0_attn_a_hidden_states']
    _d['L0_attn_a_hidden_states'] = jax.random.normal(jax.random.fold_in(jax.random.key(seed), 1), (2, 1024, 256), dtype=_x0.dtype)
    del _x0
    return _d

def reference(L0_attn_a_hidden_states, L0_attn_a_Wq, L0_attn_a_Wk, L0_attn_a_Wv, L0_attn_a_conv_q, L0_attn_a_conv_k, L0_attn_a_conv_v, L0_attn_a_A_log, L0_attn_a_Wfa, L0_attn_a_Wfb, L0_attn_a_dt_bias, L0_attn_a_Wb, L0_attn_a_Wga, L0_attn_a_Wgb, L0_attn_a_norm_w, L0_attn_a_Wo, L0_attn_b_norm_w, L0_attn_b_in_proj_w, L0_attn_b_conv_w, L0_attn_b_conv_b, L0_attn_b_x_proj_w, L0_attn_b_dt_w, L0_attn_b_dt_b, L0_attn_b_A_log, L0_attn_b_D_param, L0_attn_b_out_proj_w, L0_ffn_w_gate, L0_ffn_w_up, L0_ffn_w_down):

    def _L0_attn_a_ref(hidden_states, Wq, Wk, Wv, conv_q, conv_k, conv_v, A_log, Wfa, Wfb, dt_bias, Wb, Wga, Wgb, norm_w, Wo):
        import jax, jax.numpy as jnp
        import numpy as np
        B, T, HID = (2, 256, 256)
        H, DK, DV = (16, 128, 128)
        KC = 4
        EPS = 1e-06

        def short_conv(x, w):
            Tn = x.shape[1]
            xp = jnp.pad(x, ((0, 0), (KC - 1, 0), (0, 0)))
            out = xp[:, 0:Tn, :] * w[:, 0]
            for i in range(1, KC):
                out = out + xp[:, i:i + Tn, :] * w[:, i]
            return jax.nn.silu(out)

        def _l2norm(x):
            x = x.astype(jnp.float32)
            return x * jax.lax.rsqrt(jnp.sum(x * x, -1, keepdims=True) + 1e-06)
        Bn, Tn, _ = hidden_states.shape
        q = short_conv(hidden_states @ Wq, conv_q).reshape(Bn, Tn, H, DK)
        k = short_conv(hidden_states @ Wk, conv_k).reshape(Bn, Tn, H, DK)
        v = short_conv(hidden_states @ Wv, conv_v).reshape(Bn, Tn, H, DV)
        g = (hidden_states @ Wfa @ Wfb).astype(jnp.float32)
        g = g.reshape(Bn, Tn, H, DV) + dt_bias.astype(jnp.float32).reshape(1, 1, H, DV)
        g = jnp.exp(-jax.nn.softplus(g) * jnp.exp(A_log.astype(jnp.float32)))
        beta = jax.nn.sigmoid((hidden_states @ Wb).astype(jnp.float32))
        q = _l2norm(q) * DK ** (-0.5)
        k = _l2norm(k)
        vf = v.astype(jnp.float32)

        def step(S, inp):
            qt, kt, vt, gt, bt = inp
            S = S * gt[..., None]
            pred = jnp.einsum('bhk,bhkv->bhv', kt, S)
            delta = (vt - pred) * bt[..., None]
            S = S + kt[..., None] * delta[:, :, None, :]
            o = jnp.einsum('bhk,bhkv->bhv', qt, S)
            return (S, o)
        tfirst = lambda x: jnp.moveaxis(x, 1, 0)
        S0 = jnp.zeros((Bn, H, DK, DV), jnp.float32)
        _, o = jax.lax.scan(step, S0, (tfirst(q), tfirst(k), tfirst(vf), tfirst(g), tfirst(beta)))
        o = jnp.moveaxis(o, 0, 1)
        g2 = (hidden_states @ Wga @ Wgb).reshape(Bn, Tn, H, DV).astype(jnp.float32)
        normed = o * jax.lax.rsqrt(jnp.mean(o * o, -1, keepdims=True) + EPS) * norm_w
        o = normed * jax.nn.sigmoid(g2)
        o = o.reshape(Bn, Tn, H * DV).astype(hidden_states.dtype)
        return o @ Wo

    def _L0_attn_b_ref(x, norm_w, in_proj_w, conv_w, conv_b, x_proj_w, dt_w, dt_b, A_log, D_param, out_proj_w):
        import jax, jax.numpy as jnp
        import numpy as np
        D_MODEL = 256
        STATE = 16
        KCONV = 4
        EXPAND = 2
        D_INNER = D_MODEL * EXPAND
        EPS = 1e-05

        def _silu(v):
            return v * jax.nn.sigmoid(v)
        residual = x
        xn = x * jax.lax.rsqrt(jnp.mean(x * x, axis=-1, keepdims=True) + EPS) * norm_w
        xz = jnp.einsum('bld,ed->ble', xn, in_proj_w)
        x_inner, z = jnp.split(xz, 2, axis=-1)
        xc = jnp.transpose(x_inner, (0, 2, 1))
        xc = jax.lax.conv_general_dilated(xc, conv_w, window_strides=(1,), padding=[(KCONV - 1, 0)], dimension_numbers=('NCH', 'OIH', 'NCH'), feature_group_count=D_INNER)
        xc = xc + conv_b[None, :, None]
        xc = _silu(jnp.transpose(xc, (0, 2, 1)))
        x_ssm = jnp.einsum('bld,ed->ble', xc, x_proj_w)
        dt = jax.nn.softplus(x_ssm[..., -1:] * dt_w[:, 0] + dt_b)
        B_p = x_ssm[..., :STATE]
        C_p = x_ssm[..., STATE:2 * STATE]
        A = -jnp.exp(A_log)
        batch = x.shape[0]
        h0 = jnp.zeros((batch, D_INNER, STATE), x.dtype)

        def step(h, inp):
            dt_t, B_t, C_t, u_t = inp
            dA = jnp.exp(dt_t[..., None] * A)
            h = dA * h + (dt_t * u_t)[..., None] * B_t[:, None, :]
            y_t = jnp.sum(h * C_t[:, None, :], axis=-1) + D_param * u_t
            return (h, y_t)
        seq_first = lambda a: jnp.swapaxes(a, 0, 1)
        _, ys = jax.lax.scan(step, h0, (seq_first(dt), seq_first(B_p), seq_first(C_p), seq_first(xc)))
        y = jnp.swapaxes(ys, 0, 1)
        y = y * _silu(z)
        return jnp.einsum('ble,de->bld', y, out_proj_w) + residual

    def _L0_ffn_ref(x, w_gate, w_up, w_down):
        import jax, jax.numpy as jnp
        import numpy as np
        DIM_IN = 256
        DIM_HIDDEN = 1024
        gate = jnp.einsum('bsd,hd->bsh', x, w_gate)
        up = jnp.einsum('bsd,hd->bsh', x, w_up)
        gated = jax.nn.silu(gate) * up
        return jnp.einsum('bsh,dh->bsd', gated, w_down)
    x = L0_attn_a_hidden_states
    x = x + _L0_attn_a_ref(_layernorm(x, axis=-1), L0_attn_a_Wq, L0_attn_a_Wk, L0_attn_a_Wv, L0_attn_a_conv_q, L0_attn_a_conv_k, L0_attn_a_conv_v, L0_attn_a_A_log, L0_attn_a_Wfa, L0_attn_a_Wfb, L0_attn_a_dt_bias, L0_attn_a_Wb, L0_attn_a_Wga, L0_attn_a_Wgb, L0_attn_a_norm_w, L0_attn_a_Wo)
    x = x + _L0_ffn_ref(_layernorm(x, axis=-1), L0_ffn_w_gate, L0_ffn_w_up, L0_ffn_w_down)
    x = x + _L0_attn_b_ref(_layernorm(x, axis=-1), L0_attn_b_norm_w, L0_attn_b_in_proj_w, L0_attn_b_conv_w, L0_attn_b_conv_b, L0_attn_b_x_proj_w, L0_attn_b_dt_w, L0_attn_b_dt_b, L0_attn_b_A_log, L0_attn_b_D_param, L0_attn_b_out_proj_w)
    x = x + _L0_ffn_ref(_layernorm(x, axis=-1), L0_ffn_w_gate, L0_ffn_w_up, L0_ffn_w_down)
    return x

_drawn_inputs = setup_inputs


def setup_inputs(seed=0):
    import zlib

    import numpy as np

    out = dict(_drawn_inputs(seed))
    spreads = {'L0_attn_a_dt_bias': (0.0, 0.8),
     'L0_attn_a_norm_w': (1.0, 0.568),
     'L0_attn_b_norm_w': (1.0, 0.6),
     'L0_attn_b_conv_b': (0.0, 0.8),
     'L0_attn_b_dt_b': (0.0, 0.8),
     'L0_attn_b_D_param': (1.0, 0.6)}
    factors = {'L0_attn_a_Wfa': 8.0,
     'L0_attn_a_Wfb': 8.0,
     'L0_attn_a_Wb': 2.994,
     'L0_attn_a_Wga': 8.0,
     'L0_attn_a_Wgb': 8.0,
     'L0_attn_b_in_proj_w': 8.0,
     'L0_attn_b_conv_w': 8.0,
     'L0_attn_b_x_proj_w': 8.0,
     'L0_attn_b_dt_w': 8.0,
     'L0_attn_b_A_log': 8.0,
     'L0_attn_b_out_proj_w': 8.0}
    for name, (base, spread) in spreads.items():
        noise = np.random.default_rng([zlib.crc32(name.encode()), seed]).standard_normal(out[name].shape)
        drawn = base * np.exp(spread * noise) if base else spread * noise
        out[name] = jnp.asarray(drawn.astype(out[name].dtype))
    for name, factor in factors.items():
        out[name] = (out[name] * factor).astype(out[name].dtype)
    return out
```

```python
from contextlib import ExitStack

import concourse.bass as bass
from concourse import mybir

F32 = mybir.dt.float32
I32 = mybir.dt.int32
ALU = mybir.AluOpType
ACT = mybir.ActivationFunctionType
MUL, ADD, SUB = ALU.mult, ALU.add, ALU.subtract

P = 128
NB = 2
T = 1024
HID = 256
KT = HID // P
H = 16
KC = 4
HALO = KC - 1
CH = 64
SUBB = CH // 2
SEG = 512
NSEG = T // SEG
NC = SEG // CH
FF = 1024
DI = 512
DT = DI // P
NS = 16
NX = 2 * NS + 1
LEVELS = [1, 2, 4, 8, 16]
BANK = 512


class Lane:

    def __init__(self, sem, one_by_one=False):
        self.sem, self.count, self.program, self.waited = sem, 0, [], {}
        self.one_by_one = one_by_one

    def wait(self, *marks):
        need = {}
        for mark in marks:
            if isinstance(mark, list):
                for m in mark:
                    if m is not None:
                        need[m[0]] = max(need.get(m[0], 0), m[1])
            elif mark is not None:
                need[mark[0]] = max(need.get(mark[0], 0), mark[1])
        for sem, value in need.items():
            if self.waited.get(sem, 0) < value:
                self.waited[sem] = value
                self.program.append(lambda eng, sem=sem, value=value: eng.wait_ge(sem, value))

    def do(self, steps, *after):
        self.wait(*after)
        if not isinstance(steps, list):
            steps = [steps]
        if self.one_by_one:
            for step in steps[:-1]:
                self.wait((self.sem, self.count))
                self.count += 1
                self.program.append(lambda eng, step=step: step(eng).then_inc(self.sem, 1))
            self.wait((self.sem, self.count))
        else:
            self.program += steps[:-1]
        self.count += 1
        self.program.append(lambda eng, last=steps[-1]: last(eng).then_inc(self.sem, 1))
        return (self.sem, self.count)

    def play(self, eng):
        for step in self.program:
            step(eng)


def spread(ap, axis, n):
    a = ap.unsqueeze(axis)
    shape = list(a.shape)
    shape[axis] = n
    return a.broadcast_to(shape)


def braid(streams, lengths):
    live = [[name, gen, 0] for name, gen in streams]
    while live:
        item = min(live, key=lambda it: it[2] / lengths.get(it[0], 50))
        try:
            next(item[1])
            item[2] += 1
        except StopIteration:
            lengths[item[0]] = max(item[2], 1)
            live.remove(item)


def hybrid_block(nc, a, out):
    ctx = ExitStack()
    with ctx:
        def sb(name, shape, dt=F32, scope=ctx):
            return scope.enter_context(nc.sbuf_tensor(name, shape, dt))

        def sem(name):
            return ctx.enter_context(nc.semaphore(name))

        pe, dve, act, pool, sp = (Lane(sem("done_" + n), n == "gpsimd")
                                  for n in ("tensor", "vector", "scalar", "gpsimd", "sync"))
        psum = [ctx.enter_context(nc.psum_tensor(f"bank{i}", [P, BANK], F32)) for i in range(8)]
        bank_free = [None] * 8

        dma_total = {}

        def load(queue, name, pairs, *after):
            if name not in dma_total:
                dma_total[name] = [sem("dma_" + name), 0]
            entry = dma_total[name]
            queue.wait(*after)
            for dst, src in pairs:
                entry[1] += 16
                queue.program.append(lambda eng, d=dst, s=src, q=entry[0]: eng.dma_start(d, s).then_inc(q, 16))
            return (entry[0], entry[1])

        xT = sb("xT", [P, KT, NB * T])
        mean_w = sb("mean_w", [P, P])
        ones = sb("ones", [P, P])
        eye = sb("eye", [P, P])
        biases = sb("biases", [P, 4])
        cen = sb("cen", [P, KT, SEG])
        sq = sb("sq", [P, KT, SEG])

        loaded_x = load(sp, "x", [(xT[:, :, :], a["xT"])])
        loaded_eye = load(sp, "eye", [(eye[:, :], a["eye"])])
        const_ready = pool.do([lambda e: e.memset(mean_w[:, :], 1.0 / HID),
                               lambda e: e.memset(ones[:, :], 1.0),
                               lambda e: e.memset(biases[:, 0:1], 1e-5),
                               lambda e: e.memset(biases[:, 1:2], 1e-6),
                               lambda e: e.memset(biases[:, 2:3], 1.0),
                               lambda e: e.memset(biases[:, 3:4], P * 1e-6)])
        EPS5, EPS6, ONE, EPSQ = (biases[:, i:i + 1] for i in range(4))

        def mm(bank_ap, lhsT, rhs, start=True, stop=True, loose=False):
            return lambda e: e.matmul(bank_ap, lhsT, rhs, start=start, stop=stop, skip_group_check=loose)

        def tt(o, x, y, op):
            return lambda e: e.tensor_tensor(o, x, y, op)

        def fn(o, i, f, **kw):
            return lambda e: e.activation(o, i, f, **kw)

        norm_free = [None, None]

        def normalise(src, dst, banks, center, ready, dst_free, rstd, weight=None):
            b0, b1 = banks
            if center:
                summed = pe.do([mm(psum[b0][:, :], mean_w[:, :], src[:, k, :], k == 0, k == KT - 1)
                                for k in range(KT)], ready, const_ready, bank_free[b0])
                yield
                centred = dve.do(tt(cen[:, :, :], src, spread(psum[b0][:, :], 1, KT), SUB), summed, norm_free[0])
                bank_free[b0] = centred
                base = cen[:, :, :]
            else:
                centred, base = ready, src
            yield
            squared = act.do(fn(sq[:, :, :], base, ACT.Square), centred, norm_free[1])
            yield
            varied = pe.do([mm(psum[b1][:, :], mean_w[:, :], sq[:, k, :], k == 0, k == KT - 1)
                            for k in range(KT)], squared, const_ready, bank_free[b1])
            norm_free[1] = varied
            yield
            root = act.do(fn(rstd, psum[b1][:, :], ACT.Sqrt, bias=EPS5), varied, norm_free[0])
            bank_free[b1] = root
            yield
            inv = dve.do(lambda e: e.reciprocal(rstd, rstd), root)
            if weight is None:
                done = dve.do(tt(dst, base, spread(rstd, 1, KT), MUL), inv, dst_free)
            else:
                done = dve.do([lambda e, k=k: e.scalar_tensor_tensor(
                    dst[:, k, :], base[:, k, :], weight[:, k:k + 1], rstd, MUL, MUL)
                    for k in range(KT)], inv, dst_free)
            norm_free[0] = done
            normalise.done = done
            yield

        with ExitStack() as att:
            def sa(name, shape, dt=F32):
                return sb(name, shape, dt, att)

            xn = sa("xn", [P, KT, NB, T])
            hfa = sa("hfa", [P, NB, T])
            hga = sa("hga", [P, NB, T])
            wfa = sa("wfa", [P, KT, P])
            wga = sa("wga", [P, KT, P])
            wb = sa("wb", [P, KT, H])
            masks = sa("masks", [P, 6, SUBB])
            taps = sa("taps", [P, H, 3, KC])
            dt_bias = sa("dt_bias", [P, H])
            neg_a = sa("neg_a", [P, H])
            norm_w = sa("norm_w", [P, 1])
            beta = sa("beta", [P, T // CH, H])
            tails = sa("tails", [P, H, 3, NB, HALO])
            W = [sa(f"W{i}", [P, 7 * P]) for i in range(2)]
            WO = [sa(f"WO{i}", [P, P + HID]) for i in range(2)]
            raw = [sa(f"raw{i}", [P, NB, HALO + SEG]) for i in range(2)]
            vc = sa("vc", [P, NC, NB, CH])
            tmp, tmp2 = cen, sq
            qn = [sa(f"qn{i}", [P, NC, NB, CH]) for i in range(2)]
            kL = [sa(f"kL{i}", [P, NC, NB, CH]) for i in range(2)]
            gate = [sa(f"gate{i}", [P, NC, NB, CH]) for i in range(2)]
            R = [sa(f"R{i}", [P, 2, NC, NB, CH]) for i in range(2)]
            vT = [sa(f"vT{i}", [P, NC, P]) for i in range(3)]
            kT = [sa(f"kT{i}", [P, NC, P]) for i in range(2)]
            tot = {2 * h: sa(f"tot{2 * h}", [P, NB * SEG // (2 * h)]) for h in LEVELS}
            tot_chunk = [sa(f"tot_chunk{i}", [P, NC, NB]) for i in range(2)]
            Bd = sa("Bd", [P, NC, P])
            Od = sa("Od", [P, NC, P])
            Xd = sa("Xd", [P, NC, P])
            Bt = sa("Bt", [P, NC, P])
            Ot = Bt
            Xfull = [sa(f"Xfull{i}", [P, NC, P]) for i in range(2)]
            XX = sa("XX", [P, 2, NC, SUBB])
            Oc = sa("Oc", [P, NC, SUBB])
            bm = sa("bm", [P, NC, SUBB])
            Ac = sa("Ac", [P, NC, SUBB])
            AT = [sa(f"AT{i}", [P, NC, CH]) for i in range(2)]
            S = sa("S", [P, H, NB, P])
            Sx = sa("Sx", [P, NB, P])
            res = sa("res", [P, P])
            dpad = [sa(f"dpad{i}", [P, NB, P]) for i in range(2)]
            oT = sa("oT", [P, NC, NB, CH])

            PROJ = (0, 1)
            PROD, INV, CHAIN, SUPD = 2, 3, 4, 5
            OUT = (6, 7)
            turn = [0]

            def flat(t):
                return t[:, :, :, :].rearrange("p c b t -> p (c b t)")

            def halves(t):
                return flat(t).rearrange("p (a n) -> p a n", a=2)

            def pair_cols(t, c):
                return t[:, c, :, :].rearrange("p b t -> p (b t)")

            def half_cols(t, seg, a):
                base = seg * SEG + a * 4 * CH
                return t[:, :, base:base + 4 * CH].rearrange("p b (c t) -> p c b t", t=CH)

            def proj_bank():
                turn[0] += 1
                return PROJ[turn[0] % 2]

            small = load(sp, "small", [(wfa[:, :, :], a["wfa"]), (wga[:, :, :], a["wga"]), (wb[:, :, :], a["wb"]),
                                       (masks[:, :, :], a["masks"]), (taps[:, :, :, :], a["taps"]),
                                       (dt_bias[:, :], a["dt_bias"]), (neg_a[:, :], a["a_log"]),
                                       (norm_w[:, :], a["norm_w"])])
            w_loaded, wo_loaded, w_free, wo_free = {}, {}, [None, None], [None, None]

            def load_head(g):
                h = g % H
                w_loaded[g] = load(sp, f"w{g % 2}", [(W[g % 2][:, :], a["head_w"][h])], w_free[g % 2])

            load_head(0)

            zeroed = pool.do([lambda e, t=t: e.memset(t[:, :, :], 0.0)
                              for t in [Bd, Od, Xd, Bt, Xfull[0], Xfull[1], AT[0], AT[1], dpad[0], dpad[1]]])
            s_zeroed = dve.do(lambda e: e.memset(S[:, :, :, :], 0.0))
            expa = act.do(fn(neg_a[:, :], neg_a[:, :], ACT.Exp), small)
            a_ready = dve.do(lambda e: e.tensor_scalar(neg_a[:, :], neg_a[:, :], -1.0, None, MUL), expa)

            xn_ready = []
            xflat = xn[:, :, :, :].rearrange("p k b t -> p k (b t)")
            for n in range(NB * T // SEG):
                cols = slice(n * SEG, (n + 1) * SEG)
                for _ in normalise(xT[:, :, cols], xflat[:, :, cols],
                                   (2 * (n % 2), 2 * (n % 2) + 1), True, loaded_x, None,
                                   vc[:, 0:NC // NB, :, :].rearrange("p c b t -> p (c b t)")):
                    pass
                xn_ready.append(normalise.done)
                for w, dst in ((wfa, hfa), (wga, hga)):
                    bank = 4 + (turn[0] % 4)
                    turn[0] += 1
                    m = pe.do([mm(psum[bank][:, :], w[:, k, :], xflat[:, k, cols], k == 0, k == KT - 1)
                               for k in range(KT)], xn_ready[-1], small, bank_free[bank])
                    wide = dst[:, :, :].rearrange("p b t -> p (b t)")
                    bank_free[bank] = act.do(fn(wide[:, cols], psum[bank][:, :], ACT.Copy), m)
                    shared_ready = bank_free[bank]
            logits = pe.do([mm(psum[0][b * CH:(b + 1) * CH, c * H:(c + 1) * H], xn[:, k, b, c * CH:(c + 1) * CH],
                               wb[:, k, :], k == 0, k == KT - 1)
                            for c in range(T // CH) for b in range(NB) for k in range(KT)],
                           xn_ready, small, bank_free[0])
            beta_ready = act.do(fn(beta[:, :, :].rearrange("p c h -> p (c h)"), psum[0][:, 0:T // CH * H],
                                   ACT.Sigmoid), logits)
            bank_free[0] = beta_ready

            front_done, tree_done, state_done = {}, {}, {}
            raw_free = [None, None]
            last = {"tree": None, "oT": None, "small": None}
            last["tmp"] = last["tmp2"] = last["vc"] = list(norm_free)

            def front(g):
                seg, h = divmod(g, H)
                s = g % 2
                if g + 1 < NSEG * H:
                    load_head(g + 1)
                w = W[s]
                cols = slice(seg * SEG, (seg + 1) * SEG)
                dsts = (qn[s], kL[s], vc)
                silued = [None] * 3
                slot_free = tree_done.get(g - 2, None)
                for kind in range(3):
                    rb = (3 * g + kind) % 2
                    if seg == 0:
                        halo = pool.do(lambda e, rb=rb: e.memset(raw[rb][:, :, 0:HALO], 0.0), raw_free[rb])
                    else:
                        halo = pool.do(lambda e, rb=rb, kind=kind: e.tensor_copy(raw[rb][:, :, 0:HALO],
                                                                                tails[:, h, kind, :, :]), raw_free[rb])
                    evac = []
                    for b in range(NB):
                        bank = proj_bank()
                        m = pe.do([mm(psum[bank][:, :], w[:, (kind * KT + k) * P:(kind * KT + k + 1) * P],
                                      xn[:, k, b, cols], k == 0, k == KT - 1) for k in range(KT)],
                                  w_loaded[g], xn_ready, bank_free[bank])
                        evac.append(act.do(fn(raw[rb][:, b, HALO:], psum[bank][:, :], ACT.Copy), m, raw_free[rb]))
                        bank_free[bank] = evac[-1]
                        yield
                    kept = None
                    if seg == 0:
                        kept = pool.do(lambda e, rb=rb, kind=kind: e.tensor_copy(
                            tails[:, h, kind, :, :], raw[rb][:, :, SEG:SEG + HALO]), evac)
                    tap = lambda i, kind=kind: taps[:, h, kind, i:i + 1]
                    conv = dsts[kind][:, :, :, :].rearrange("p c b t -> p b c t")
                    shifted = lambda i, rb=rb: raw[rb][:, :, i:i + SEG].rearrange("p b (c t) -> p b c t", t=CH)
                    m = dve.do(lambda e, shifted=shifted, tap=tap, conv=conv: e.tensor_scalar(
                        conv, shifted(0), tap(0), None, MUL), evac, halo, small,
                        last["vc"] if kind == 2 else slot_free)
                    for i in range(1, KC):
                        m = dve.do([lambda e, i=i, b=b, shifted=shifted, tap=tap, conv=conv: e.scalar_tensor_tensor(
                            conv[:, b, :, :], shifted(i)[:, b, :, :], tap(i), conv[:, b, :, :], MUL, ADD)
                            for b in range(NB)], m)
                    raw_free[rb] = [m, kept]
                    yield
                    silued[kind] = act.do(fn(dsts[kind][:, :, :, :], dsts[kind][:, :, :, :], ACT.Silu), m)
                    yield
                vt_free = state_done.get(g - 3, None)
                turned = []
                for half in range(2):
                    bank = proj_bank()
                    m = pe.do([lambda e, c=c, bank=bank: e.transpose(
                        psum[bank][:, (c % 4) * P:(c % 4 + 1) * P], pair_cols(vc, c), eye[:, :])
                        for c in range(4 * half, 4 * half + 4)], silued[2], loaded_eye, bank_free[bank])
                    last["vc"] = m
                    turned.append(dve.do(lambda e, bank=bank, half=half: e.tensor_copy(
                        vT[g % 3][:, 4 * half:4 * half + 4, :].rearrange("p c d -> p (c d)"), psum[bank][:, :]),
                        m, vt_free))
                    bank_free[bank] = turned[-1]
                    yield
                normed = []
                for kind, scale, eps in ((0, float(P), EPSQ), (1, 1.0, EPS6)):
                    t = halves(dsts[kind])
                    squared = act.do(fn(tmp[:, :, :], t, ACT.Square), silued[kind], last["tmp"])
                    logs = []
                    for b in range(NB):
                        bank = proj_bank()
                        m = pe.do(mm(psum[bank][:, :], ones[:, :], tmp[:, b, :]), squared, const_ready,
                                  bank_free[bank])
                        last["tmp"] = m
                        logs.append(act.do(fn(tmp2[:, b, :], psum[bank][:, :], ACT.Ln, bias=eps, scale=scale), m,
                                           last["tmp2"]))
                        bank_free[bank] = logs[-1]
                        yield
                    inv = act.do(fn(tmp2[:, :, :], tmp2[:, :, :], ACT.Exp, scale=-0.5), logs)
                    m = dve.do(tt(t, t, tmp2[:, :, :], MUL), inv)
                    last["tmp2"] = m
                    normed.append(m)
                    yield
                absd, relud = [], []
                for b in range(NB):
                    bank = proj_bank()
                    m = pe.do(mm(psum[bank][:, :], w[:, 6 * P:7 * P], half_cols(hfa, seg, b)), w_loaded[g], shared_ready,
                              bank_free[bank])
                    absd.append(act.do(fn(tmp[:, b, :], psum[bank][:, :], ACT.Abs, bias=dt_bias[:, h:h + 1]), m,
                                       last["tmp"]))
                    w_free[s] = m
                    relud.append(dve.do(lambda e, b=b, bank=bank: e.tensor_scalar(
                        halves(gate[s])[:, b, :], psum[bank][:, :], dt_bias[:, h:h + 1], 0.0, ADD, ALU.max),
                        absd[-1], slot_free))
                    bank_free[bank] = relud[-1]
                    yield
                m = act.do(fn(tmp2[:, :, :], tmp[:, :, :], ACT.Exp, scale=-1.0), absd, last["tmp2"])
                last["tmp"] = m
                m = act.do(fn(tmp2[:, :, :], tmp2[:, :, :], ACT.Ln, bias=ONE), m)
                yield
                m = dve.do(tt(halves(gate[s]), halves(gate[s]), tmp2[:, :, :], ADD), m, relud)
                last["tmp2"] = m
                m = act.do(fn(flat(gate[s]), flat(gate[s]), ACT.Exp, scale=neg_a[:, h:h + 1]), m, a_ready)
                front_done[g] = normed + turned + [m]
                yield

            def tree(g):
                seg, h = divmod(g, H)
                s = g % 2
                ready = front_done[g]
                r_free = state_done.get(g - 2, None)
                wo_loaded[g] = load(sp, f"wo{s}", [(WO[s][:, :], a["out_w"][h])], wo_free[s])
                Rf = R[s][:, :, :, :, :].rearrange("p a c b t -> p a (c b t)")
                Lf = flat(kL[s])
                beta_g = beta[:, seg * NC:(seg + 1) * NC, h]
                bank = PROD

                def quad(w):
                    return slice(SUBB * w, SUBB * (w + 1))

                def block(t, c, b, u):
                    return t[:, c, b, u * SUBB:(u + 1) * SUBB]

                def block_r(c, b, u):
                    return R[s][:, :, c, b, u * SUBB:(u + 1) * SUBB]

                prod = pe.do([mm(psum[bank][quad(2 * b + u), c * SUBB:(c + 1) * SUBB], block(kL[s], c, b, u),
                                 block(qn[s], c, b, u)) for c in range(NC) for b in range(NB) for u in range(2)],
                             ready, bank_free[bank])
                m = dve.do(tt(Ac[:, :, :], psum[bank][:, 0:NC * SUBB].rearrange("p (c i) -> p c i", c=NC),
                              spread(masks[:, 0, :], 1, NC), MUL), prod, small, last["tree"])
                bank_free[bank] = m
                acc = m
                yield
                rk = pool.do(tt(Rf[:, 0, :], Lf, flat(gate[s]), MUL), ready, r_free)
                rq = dve.do(tt(Rf[:, 1, :], flat(qn[s]), flat(gate[s]), MUL), ready, r_free)
                r_ready, l_ready = [rk, rq], ready
                t_ready, t_now = ready, flat(gate[s])
                yield
                x_free = last["tree"]
                for li, half in enumerate(LEVELS):
                    prod = pe.do([mm(psum[bank][quad(2 * b + u), c * CH:(c + 1) * CH], block(kL[s], c, b, u),
                                     block_r(c, b, u)) for c in range(NC) for b in range(NB)
                                  for u in range(2)], r_ready, l_ready, bank_free[bank])
                    view = psum[bank][:, :].rearrange("p (c a i) -> p c a i", c=NC, a=2)
                    bmd = pool.do(tt(bm[:, :, :], spread(masks[:, 1 + li, :], 1, NC), spread(beta_g, 2, SUBB), MUL),
                                  beta_ready, small, last["small"])
                    yield
                    nb = NB * SEG // (2 * half)
                    pair = t_now.rearrange("p (n two) -> p n two", two=2)
                    Rv = Rf.rearrange("p a (n two t) -> p a n two t", two=2, t=half)
                    Lv = Lf.rearrange("p (n two t) -> p n two t", two=2, t=half)
                    up_r = dve.do([lambda e, x=x, Rv=Rv, pair=pair, half=half: e.tensor_tensor(
                        Rv[:, x, :, 1, :], Rv[:, x, :, 1, :], spread(pair[:, :, 0], 2, half), MUL)
                        for x in range(2)], prod, t_ready)
                    up_l = pool.do(tt(Lv[:, :, 0, :], Lv[:, :, 0, :], spread(pair[:, :, 1], 2, half), MUL),
                                   prod, t_ready)
                    up_t = pool.do(tt(tot[2 * half][:, :], pair[:, :, 0], pair[:, :, 1], MUL), t_ready, last["tree"])
                    r_ready, l_ready, t_ready, t_now = up_r, up_l, up_t, tot[2 * half][:, :]
                    yield
                    bd = dve.do([tt(Bd[quad(w), :, quad(w)], view[quad(w), :, 0, :], bm[quad(w), :, :], MUL)
                                 for w in range(4)], prod, bmd, zeroed, x_free)
                    if half == 1:
                        bk_done = dve.do(tt(XX[:, 1, :, :], view[:, :, 0, :], bm[:, :, :], MUL), bmd, x_free)
                        bd_or = [bd, bk_done]
                    else:
                        bd_or = bd
                    acc = dve.do(lambda e, li=li, view=view: e.copy_predicated(
                        Ac[:, :, :], spread(masks[:, 1 + li, :], 1, NC).bitcast(I32), view[:, :, 1, :]), acc, prod)
                    bank_free[bank] = acc
                    last["small"] = bd_or
                    yield
                    if half == 1:
                        p1 = pe.do([mm(psum[INV][:, c * SUBB:(c + 1) * SUBB], Bd[:, c, :], masks[:, 0, :])
                                    for c in range(NC)], bd, bank_free[INV])
                        i_b = spread(masks[:, 0, :], 1, NC)
                        x0 = dve.do(tt(XX[:, 0, :, :], i_b,
                                       psum[INV][:, 0:NC * SUBB].rearrange("p (c i) -> p c i", c=NC), SUB), p1, x_free)
                        bank_free[INV] = x0
                        xs = dve.do(tt(XX[:, 1, :, :], i_b, XX[:, 1, :, :], SUB), bk_done)
                        x_free = p1
                    else:
                        p1 = pe.do([mm(psum[INV][:, c * SUBB:(c + 1) * SUBB], Bd[:, c, :], XX[:, 0, c, :])
                                    for c in range(NC)], bd, xs, bank_free[INV])
                        pv = psum[INV][:, 0:NC * SUBB].rearrange("p (c i) -> p c i", c=NC)
                        od = act.do([fn(Oc[:, :, :], pv, ACT.Copy)] +
                                    [fn(Od[quad(w), :, quad(w)], pv[quad(w), :, :], ACT.Copy) for w in range(4)],
                                    p1, zeroed, x_free)
                        yield
                        p2 = pe.do([mm(psum[INV][:, c * SUBB:(c + 1) * SUBB], Xd[:, c, :], Oc[:, c, :])
                                    for c in range(NC)] +
                                   [mm(psum[INV][:, (NC + c) * SUBB:(NC + c + 1) * SUBB], Od[:, c, :], XX[:, 1, c, :])
                                    for c in range(NC)], od, xd)
                        xs = dve.do(tt(XX[:, :, :, :].rearrange("p a c i -> p (a c i)"),
                                       XX[:, :, :, :].rearrange("p a c i -> p (a c i)"), psum[INV][:, :], SUB), p2)
                        bank_free[INV] = xs
                        x_free = p2
                    target = Xd if half < LEVELS[-1] else Xfull[s]
                    xd = pool.do([lambda e, w=w, target=target: e.tensor_copy(target[quad(w), :, quad(w)],
                                                                             XX[quad(w), 1, :, :])
                                  for w in range(4)], xs, zeroed, x_free, r_free)
                    yield
                prod = pe.do([mm(psum[bank][quad(2 * b), c * CH:(c + 1) * CH], block(kL[s], c, b, 0),
                                 block_r(c, b, 1)) for c in range(NC) for b in range(NB)],
                             r_ready, l_ready, bank_free[bank])
                view = psum[bank][:, :].rearrange("p (c a i) -> p c a i", c=NC, a=2)
                yield
                pair = t_now.rearrange("p (n two) -> p n two", two=2)
                Rv = Rf.rearrange("p a (n two t) -> p a n two t", two=2, t=SUBB)
                Lv = Lf.rearrange("p (n two t) -> p n two t", two=2, t=SUBB)
                up_r = dve.do([lambda e, x=x, Rv=Rv, pair=pair, half=half: e.tensor_tensor(
                    Rv[:, x, :, 1, :], Rv[:, x, :, 1, :], spread(pair[:, :, 0], 2, SUBB), MUL)
                    for x in range(2)], prod, t_ready)
                up_l = pool.do(tt(Lv[:, :, 0, :], Lv[:, :, 0, :], spread(pair[:, :, 1], 2, SUBB), MUL), prod, t_ready)
                up_t = pool.do(tt(tot_chunk[s][:, :, :].rearrange("p c b -> p (c b)"), pair[:, :, 0], pair[:, :, 1],
                                  MUL), t_ready, r_free)
                bt = dve.do([tt(Bt[quad(w), :, quad(w + 1)], view[quad(w), :, 0, :],
                                spread(beta_g[quad(w), :], 2, SUBB), MUL) for w in (0, 2)], prod, zeroed, beta_ready)
                at = dve.do([lambda e, w=w, view=view: e.tensor_copy(AT[s][quad(w), :, SUBB:CH],
                                                                    view[quad(w), :, 1, :]) for w in (0, 2)],
                            prod, zeroed, r_free)
                bank_free[bank] = at
                low = pool.do([lambda e, w=w: e.tensor_copy(AT[s][quad(w), :, SUBB * (w % 2):SUBB * (w % 2 + 1)],
                                                           Ac[quad(w), :, :]) for w in range(4)], acc, zeroed, r_free)
                yield
                p1 = pe.do([mm(psum[INV][:, c * SUBB:(c + 1) * SUBB], Bt[:, c, :], XX[:, 0, c, :])
                            for c in range(NC)], bt, xs, bank_free[INV])
                pv = psum[INV][:, 0:NC * SUBB].rearrange("p (c i) -> p c i", c=NC)
                ot = act.do([fn(Ot[quad(w), :, quad(w - 1)], pv[quad(w), :, :], ACT.Copy) for w in (1, 3)], p1, zeroed)
                yield
                p2 = pe.do([mm(psum[INV][:, c * SUBB:(c + 1) * SUBB], Ot[:, c, :], XX[:, 1, c, :])
                            for c in range(NC)], ot)
                xf = act.do([lambda e, w=w: e.activation(Xfull[s][quad(w), :, quad(w + 1)], pv[quad(w), :, :],
                                                         ACT.Copy, scale=-1.0) for w in (0, 2)], p2, zeroed, r_free)
                bank_free[INV] = xf
                yield
                turned = []
                for q in range(2):
                    bk2 = proj_bank()
                    m = pe.do([lambda e, c=c, bk2=bk2: e.transpose(
                        psum[bk2][:, (c % 4) * P:(c % 4 + 1) * P], pair_cols(kL[s], c), eye[:, :])
                        for c in range(4 * q, 4 * q + 4)], up_l, bank_free[bk2])
                    turned.append(act.do(fn(kT[s][:, 4 * q:4 * q + 4, :].rearrange("p c d -> p (c d)"),
                                            psum[bk2][:, :], ACT.Copy), m, r_free))
                    bank_free[bk2] = turned[-1]
                    yield
                last["tree"] = [xf, at, low, xd, p2, up_t]
                tree_done[g] = [up_r, up_t, low, at, xd, xf, p2] + turned
                yield

            s_ready = {h: [s_zeroed, s_zeroed] for h in range(H)}
            dpad_free = [None, None]
            chain = {"sx": None}
            x_added = [None] * (NB * NSEG)

            def state(g):
                seg, h = divmod(g, H)
                s = g % 2
                ready = tree_done[g]
                upd = s_ready[h]
                o_evac = []
                for c in range(NC):
                    src = S[:, h, :, :] if c % 2 == 0 else Sx[:, :, :]
                    dst = Sx[:, :, :] if c % 2 == 0 else S[:, h, :, :]
                    d = dpad[c % 2]
                    ob = OUT[c // 4]
                    ocol = lambda b, c=c: slice((c % 4) * P + b * CH, (c % 4) * P + (b + 1) * CH)
                    pred = pe.do([mm(psum[CHAIN][b * CH:(b + 1) * CH, 0:P], R[s][:, 0, c, b, :], src[:, b, :])
                                  for b in range(NB)], ready, upd, bank_free[CHAIN])
                    rdone = dve.do(tt(res[:, :], vT[g % 3][:, c, :], psum[CHAIN][:, 0:P], SUB), pred)
                    seen = pe.do([mm(psum[ob][:, ocol(b)], src[:, b, :], R[s][:, 1, c, b, :],
                                     start=(c % 4 == 0 and b == 0), stop=False, loose=True) for b in range(NB)],
                                 bank_free[ob])
                    yield
                    solved = pe.do(mm(psum[CHAIN][:, P:2 * P], Xfull[s][:, c, :], res[:, :]), rdone)
                    dd = act.do([lambda e, b=b, d=d, c=c: e.activation(
                        d[b * CH:(b + 1) * CH, b, :], psum[CHAIN][b * CH:(b + 1) * CH, P:2 * P], ACT.Copy,
                        scale=beta[b * CH:(b + 1) * CH, seg * NC + c, h:h + 1]) for b in range(NB)],
                        solved, beta_ready, zeroed, dpad_free[c % 2])
                    bank_free[CHAIN] = dd
                    yield
                    outer = pe.do(mm(psum[SUPD][:, 0:NB * P], kT[s][:, c, :], d[:, :, :].rearrange("p b v -> p (b v)")),
                                  dd, bank_free[SUPD])
                    upd = dve.do([lambda e, b=b, src=src, dst=dst, c=c: e.scalar_tensor_tensor(
                        dst[:, b, :], src[:, b, :], tot_chunk[s][:, c, b:b + 1], psum[SUPD][:, b * P:(b + 1) * P],
                        MUL, ADD) for b in range(NB)], outer, seen)
                    bank_free[SUPD] = upd
                    within = pe.do([mm(psum[ob][:, ocol(b)], d[:, b, :], AT[s][:, c, :], start=False, stop=True,
                                       loose=True) for b in range(NB)])
                    dpad_free[c % 2] = within
                    if c % 4 == 3:
                        k = c // 4
                        m = act.do(fn(halves(oT)[:, k, :], psum[ob][:, :], ACT.Copy), within, last["oT"])
                        bank_free[ob] = m
                        o_evac.append(m)
                    yield
                s_ready[h] = upd
                tmp3, tmp4 = (R[s][:, x, :, :, :].rearrange("p c b t -> p (c b t)").rearrange(
                    "p (a n) -> p a n", a=2) for x in range(2))
                last["tmp3"] = last["tmp4"] = within
                oh = halves(oT)
                squared = act.do(fn(tmp3[:, :, :], oh, ACT.Square), o_evac, last["tmp3"])
                logs = []
                for b in range(NB):
                    bank = proj_bank()
                    m = pe.do(mm(psum[bank][:, :], ones[:, :], tmp3[:, b, :]), squared, bank_free[bank])
                    last["tmp3"] = m
                    logs.append(act.do(fn(tmp4[:, b, :], psum[bank][:, :], ACT.Ln, bias=EPS6, scale=1.0 / P), m,
                                       last["tmp4"]))
                    bank_free[bank] = logs[-1]
                inv = act.do(fn(tmp4[:, :, :], tmp4[:, :, :], ACT.Exp, scale=-0.5), logs)
                m = dve.do(lambda e: e.scalar_tensor_tensor(oh, oh, norm_w[:, 0:1], tmp4[:, :, :],
                                                            MUL, MUL), inv)
                last["tmp4"] = m
                normed = m
                yield
                exps = []
                for b in range(NB):
                    bank = proj_bank()
                    m = pe.do(mm(psum[bank][:, :], WO[s][:, 0:P], half_cols(hga, seg, b)), wo_loaded[g], shared_ready,
                              bank_free[bank])
                    exps.append(act.do(fn(tmp3[:, b, :], psum[bank][:, :], ACT.Exp, scale=-1.0), m, last["tmp3"]))
                    bank_free[bank] = exps[-1]
                yield
                m = dve.do(lambda e: e.tensor_scalar(tmp3[:, :, :], tmp3[:, :, :], 1.0, None, ADD), exps)
                m = dve.do(lambda e: e.reciprocal(tmp3[:, :, :], tmp3[:, :, :]), m)
                m = dve.do(tt(oh, oh, tmp3[:, :, :], MUL), m, normed)
                last["tmp3"] = m
                gated = m
                yield
                for b in range(NB):
                    for k in range(KT):
                        bank = proj_bank()
                        m = pe.do(mm(psum[bank][:, :], WO[s][:, (k + 1) * P:(k + 2) * P], oh[:, b, :]), gated,
                                  bank_free[bank])
                        dst = half_cols(xT[:, k, :].rearrange("p (b t) -> p b t", b=NB), seg, b)
                        bank_free[bank] = dve.do(tt(dst, dst, psum[bank][:, :].rearrange(
                            "p (c b t) -> p c b t", b=NB, t=CH), ADD), m, chain.get((b, k)))
                        chain[(b, k)] = bank_free[bank]
                        x_added[seg] = x_added[NSEG + seg] = bank_free[bank]
                        yield
                last["oT"] = m
                wo_free[s] = m
                state_done[g] = [upd, within, last["tmp3"], last["tmp4"]]

            lengths = {}
            NG = NSEG * H
            for step in range(NG + 2):
                streams = []
                if step >= 2:
                    streams.append(("state", state(step - 2)))
                if 1 <= step <= NG:
                    streams.append(("tree", tree(step - 1)))
                if step < NG:
                    streams.append(("front", front(step)))
                braid(streams, lengths)

        def fence():
            marks = [(lane.sem, lane.count) for lane in (pe, dve, act, pool) if lane.count]
            for lane in (pe, dve, act, pool, sp):
                lane.wait(marks)
            return marks

        def swiglu(tag, x_ready):
            with ExitStack() as ff:
                wg = sb("wg" + tag, [P, KT, FF], F32, ff)
                wu = sb("wu" + tag, [P, KT, FF], F32, ff)
                wd = sb("wd" + tag, [P, FF // P, HID], F32, ff)
                xh = [sb(f"xh{i}" + tag, [P, KT, SEG], F32, ff) for i in range(2)]
                hid = [sb(f"hid{i}" + tag, [P, FF // P, SEG], F32, ff) for i in range(2)]
                rstd = sb("rstd" + tag, [P, SEG], F32, ff)
                sg = [sb(f"sg{i}" + tag, [P, SEG], F32, ff) for i in range(2)]
                w = load(sp, "ffn" + tag, [(wg[:, :, :], a["w_gate"]), (wu[:, :, :], a["w_up"]),
                                           (wd[:, :, :], a["w_down"])])
                xh_free, hid_free, sg_free = [None] * 2, [None] * 2, [None] * 2
                added = []
                for n in range(NB * T // SEG):
                    cols = slice(n * SEG, (n + 1) * SEG)
                    s = n % 2
                    for _ in normalise(xT[:, :, cols], xh[s][:, :, :], (6, 7), True, x_ready[n], xh_free[s],
                                       rstd[:, :]):
                        pass
                    h_ready = normalise.done
                    hdone = []
                    for j in range(FF // P):
                        bg, bu = j % 2, 2 + j % 2
                        mg = pe.do([mm(psum[bg][:, :], wg[:, k, j * P:(j + 1) * P], xh[s][:, k, :], k == 0,
                                       k == KT - 1) for k in range(KT)], w, h_ready, bank_free[bg])
                        mu = pe.do([mm(psum[bu][:, :], wu[:, k, j * P:(j + 1) * P], xh[s][:, k, :], k == 0,
                                       k == KT - 1) for k in range(KT)], bank_free[bu])
                        m = act.do(fn(sg[j % 2][:, :], psum[bg][:, :], ACT.Silu), mg, sg_free[j % 2])
                        bank_free[bg] = m
                        m = dve.do(tt(hid[s][:, j, :], sg[j % 2][:, :], psum[bu][:, :], MUL), m, mu, hid_free[s])
                        bank_free[bu] = sg_free[j % 2] = m
                        hdone.append(m)
                    xh_free[s] = mu
                    for k in range(KT):
                        bank = 4 + k
                        m = pe.do([mm(psum[bank][:, :], wd[:, j, k * P:(k + 1) * P], hid[s][:, j, :], j == 0,
                                      j == FF // P - 1) for j in range(FF // P)], hdone, bank_free[bank])
                        bank_free[bank] = dve.do(tt(xT[:, k, cols], xT[:, k, cols], psum[bank][:, :], ADD), m)
                    hid_free[s] = m
                    added.append(bank_free[4 + KT - 1])
                return added

        fence()
        x_ready = swiglu("0", x_added)
        fence()

        with ExitStack() as mb:
            def sm(name, shape, dt=F32):
                return sb(name, shape, dt, mb)

            w_in = sm("w_in", [P, KT, 2 * DI])
            w_x = sm("w_x", [P, DT, NX])
            w_o = sm("w_o", [P, DT, HID])
            m_norm = sm("m_norm", [P, KT])
            m_taps = sm("m_taps", [P, DT, KC])
            m_cb = sm("m_cb", [P, DT])
            m_dtw = sm("m_dtw", [P, DT])
            m_dtb = sm("m_dtb", [P, DT])
            m_D = sm("m_D", [P, DT])
            m_A = sm("m_A", [P, DT, NS])
            u = sm("u", [P, KT, T])
            rstd = sm("rstd", [P, SEG])
            un = [sm(f"un{i}", [P, KT, SEG]) for i in range(2)]
            mraw = sm("mraw", [P, DT, HALO + T])
            xc = sm("xc", [P, DT, T])
            zs = sm("zs", [P, DT, T])
            xs = sm("xs", [NX, T])
            dtv = sm("dtv", [P, DT, T])
            dtu = sm("dtu", [P, DT, T])
            Bn = [sm(f"Bn{i}", [P, T]) for i in range(2)]
            Cn = [sm(f"Cn{i}", [P, T]) for i in range(2)]
            dA = [sm(f"dA{i}", [P, T]) for i in range(2)]
            dBu = [sm(f"dBu{i}", [P, T]) for i in range(2)]
            hs = [sm(f"hs{i}", [P, T]) for i in range(2)]
            hc = [sm(f"hc{i}", [P, T]) for i in range(2)]

            wl = load(sp, "mamba", [(w_in[:, :, :], a["w_in"]), (w_x[:, :, :], a["w_x"]), (w_o[:, :, :], a["w_o"]),
                                    (m_norm[:, :], a["m_norm"]), (m_taps[:, :, :], a["m_taps"]),
                                    (m_cb[:, :], a["m_cb"]), (m_dtw[:, :], a["m_dtw"]), (m_dtb[:, :], a["m_dtb"]),
                                    (m_D[:, :], a["m_D"]), (m_A[:, :, :], a["m_A"])])
            e1 = act.do(fn(m_A[:, :, :], m_A[:, :, :], ACT.Exp), wl)
            m_a_ready = dve.do(lambda e: e.tensor_scalar(m_A[:, :, :], m_A[:, :, :], -1.0, None, MUL), e1)
            halo = pool.do(lambda e: e.memset(mraw[:, :, 0:HALO], 0.0))
            m_ready = [None] * (NB * NSEG)
            u_free = un_free = raw_free2 = xc_free = zs_free = None
            scan_free = None
            bn_free, cn_free = [None, None], [None, None]
            da_free, dbu_free, hs_free, hc_free = [None] * 2, [None] * 2, [None] * 2, [None] * 2
            xs_free = None
            for b in range(NB):
                u_done, evac, zdone = [], [], []
                for n in range(NSEG):
                    cols = slice(n * SEG, (n + 1) * SEG)
                    xcols = slice(b * T + n * SEG, b * T + (n + 1) * SEG)
                    for _ in normalise(xT[:, :, xcols], u[:, :, cols], (6, 7), True, x_ready[b * NSEG + n], u_free,
                                       rstd[:, :]):
                        pass
                    u_done.append(normalise.done)
                    for _ in normalise(u[:, :, cols], un[n][:, :, :], (6, 7), False, normalise.done, un_free,
                                       rstd[:, :], m_norm[:, :]):
                        pass
                    un_done = normalise.done
                    for j in range(2 * DT):
                        bank = j % 4
                        m = pe.do([mm(psum[bank][:, :], w_in[:, k, j * P:(j + 1) * P], un[n][:, k, :], k == 0,
                                      k == KT - 1) for k in range(KT)], wl, un_done, bank_free[bank])
                        if j < DT:
                            bank_free[bank] = act.do(fn(mraw[:, j, HALO + n * SEG:HALO + (n + 1) * SEG],
                                                        psum[bank][:, :], ACT.Copy), m, raw_free2)
                            evac.append(bank_free[bank])
                        else:
                            bank_free[bank] = act.do(fn(zs[:, j - DT, cols], psum[bank][:, :], ACT.Silu), m, zs_free)
                            zdone.append(bank_free[bank])
                    un_last = m
                un_free = un_last
                xdone = []
                for j in range(DT):
                    m = dve.do(lambda e, j=j: e.tensor_scalar(xc[:, j, :], mraw[:, j, 0:T], m_taps[:, j, 0:1],
                                                              None, MUL), evac, halo, wl, xc_free)
                    for i in range(1, KC):
                        m = dve.do(lambda e, j=j, i=i: e.scalar_tensor_tensor(
                            xc[:, j, :], mraw[:, j, i:i + T], m_taps[:, j, i:i + 1], xc[:, j, :], MUL, ADD), m)
                    raw_free2 = m
                    xdone.append(act.do(fn(xc[:, j, :], xc[:, j, :], ACT.Silu, bias=m_cb[:, j:j + 1]), m))
                ssm = []
                for n in range(NSEG):
                    cols = slice(n * SEG, (n + 1) * SEG)
                    m = pe.do([mm(psum[n][0:NX, :], w_x[:, j, :], xc[:, j, cols], j == 0, j == DT - 1)
                               for j in range(DT)], xdone, bank_free[n])
                    bank_free[n] = act.do(fn(xs[:, cols], psum[n][0:NX, :], ACT.Copy), m, xs_free)
                    ssm.append(bank_free[n])
                stored = load(sp, f"scratch{b}", [(a["scratch"][b], xs[:, :])], ssm)
                xs_free = stored

                def rows(name, tile, r, *after):
                    return load(sp, name, [(tile[:, :], a["scratch"][b, r:r + 1, :].broadcast_to([P, T]))], *after)

                dt_in = rows("dt", dA[0], 2 * NS, stored, da_free[0])
                for j in range(DT):
                    m = act.do(fn(dA[1][:, :], dA[0][:, :], ACT.Abs, scale=m_dtw[:, j:j + 1], bias=m_dtb[:, j:j + 1]),
                               dt_in, wl, da_free[1])
                    r1 = dve.do(lambda e, j=j: e.tensor_scalar(dtv[:, j, :], dA[0][:, :], m_dtw[:, j:j + 1],
                                                               m_dtb[:, j:j + 1], MUL, ADD), dt_in, wl, scan_free)
                    r2 = dve.do(lambda e, j=j: e.tensor_scalar(dtv[:, j, :], dtv[:, j, :], 0.0, None, ALU.max), r1)
                    m = act.do(fn(dA[1][:, :], dA[1][:, :], ACT.Exp, scale=-1.0), m)
                    m = act.do(fn(dA[1][:, :], dA[1][:, :], ACT.Ln, bias=ONE), m)
                    m = dve.do(tt(dtv[:, j, :], dtv[:, j, :], dA[1][:, :], ADD), m, r2)
                    da_free[1] = m
                    dt_done = m
                    dtu_done = dve.do(tt(dtu[:, j, :], dtv[:, j, :], xc[:, j, :], MUL), m, xdone, scan_free)
                da_free[0] = r1
                count = 0
                started = [False] * 8
                for n in range(NS):
                    bs = rows(f"B{n % 2}", Bn[n % 2], n, stored, bn_free[n % 2])
                    cs = rows(f"C{n % 2}", Cn[n % 2], NS + n, cn_free[n % 2])
                    for j in range(DT):
                        k = count % 2
                        count += 1
                        m1 = act.do(fn(dA[k][:, :], dtv[:, j, :], ACT.Exp, scale=m_A[:, j, n:n + 1]), dt_done,
                                    m_a_ready, da_free[k])
                        m2 = pool.do(tt(dBu[k][:, :], dtu[:, j, :], Bn[n % 2][:, :], MUL), dtu_done, bs, dbu_free[k])
                        m3 = dve.do(lambda e, k=k: e.tensor_tensor_scan(hs[k][:, :], dA[k][:, :], dBu[k][:, :], 0.0,
                                                                        MUL, ADD), m1, m2, hs_free[k])
                        da_free[k] = dbu_free[k] = m3
                        m4 = dve.do(tt(hc[k][:, :], hs[k][:, :], Cn[n % 2][:, :], MUL), m3, cs, hc_free[k])
                        hs_free[k] = m4
                        m5 = pe.do([mm(psum[2 * j + q][:, :], eye[:, :], hc[k][:, q * SEG:(q + 1) * SEG], n == 0,
                                       n == NS - 1, loose=True) for q in range(NSEG)], m4,
                                   [bank_free[2 * j], bank_free[2 * j + 1]] if n == 0 else None)
                        hc_free[k] = m5
                    bn_free[n % 2], cn_free[n % 2] = m2, m4
                scan_free = m3
                for j in range(DT):
                    m = dve.do([lambda e, j=j, q=q: e.scalar_tensor_tensor(
                        xc[:, j, q * SEG:(q + 1) * SEG], xc[:, j, q * SEG:(q + 1) * SEG], m_D[:, j:j + 1],
                        psum[2 * j + q][:, :], MUL, ADD) for q in range(NSEG)], m5)
                    bank_free[2 * j] = bank_free[2 * j + 1] = m
                    m = dve.do(tt(xc[:, j, :], xc[:, j, :], zs[:, j, :], MUL), m, zdone)
                zs_free = m
                for n in range(NSEG):
                    cols = slice(n * SEG, (n + 1) * SEG)
                    xcols = slice(b * T + n * SEG, b * T + (n + 1) * SEG)
                    for k in range(KT):
                        bank = n * KT + k
                        mo = pe.do([mm(psum[bank][:, :], w_o[:, j, k * P:(k + 1) * P], xc[:, j, cols], j == 0,
                                       j == DT - 1) for j in range(DT)], m, bank_free[bank])
                        bank_free[bank] = dve.do(tt(xT[:, k, xcols], xT[:, k, xcols], psum[bank][:, :], ADD), mo)
                        m_ready[b * NSEG + n] = dve.do(tt(xT[:, k, xcols], xT[:, k, xcols], u[:, k, cols], ADD),
                                                       bank_free[bank], u_done)
                    u_free = m_ready[b * NSEG + n]
                xc_free = mo

        fence()
        final = swiglu("1", m_ready)
        outs = None
        for n in range(NB * T // SEG):
            cols = slice(n * SEG, (n + 1) * SEG)
            outs = load(sp, "out", [(out[:, :, cols], xT[:, :, cols])], final[n])
        sp.wait(outs)

        block = ctx.enter_context(nc.Block())

        @block.tensor
        def _(eng):
            pe.play(eng)

        @block.vector
        def _(eng):
            dve.play(eng)

        @block.scalar
        def _(eng):
            act.play(eng)

        @block.gpsimd
        def _(eng):
            pool.play(eng)

        @block.sync
        def _(eng):
            sp.play(eng)


def kernel(**inputs):
    import numpy as np
    import concourse.bacc as bacc
    from concourse.bass_utils import run_bass_kernel_spmd

    i = {k: np.asarray(v) for k, v in inputs.items()}
    A, B, FN = "L0_attn_a_", "L0_attn_b_", "L0_ffn_"

    def rows(w):
        return w.reshape(-1, P, w.shape[1]).transpose(1, 0, 2)

    x = i[A + "hidden_states"]
    heads = np.concatenate(
        [rows(i[A + w]).reshape(P, KT, H, P).transpose(2, 0, 1, 3).reshape(H, P, KT * P) for w in ("Wq", "Wk", "Wv")] +
        [i[A + "Wfb"].reshape(P, H, P).transpose(1, 0, 2)], axis=2)
    out_w = np.concatenate([i[A + "Wgb"].reshape(P, H, P).transpose(1, 0, 2), i[A + "Wo"].reshape(H, P, HID)], axis=2)
    conv = np.stack([i[A + c].reshape(H, P, KC) for c in ("conv_q", "conv_k", "conv_v")], axis=1)
    j, col = np.arange(P)[:, None] % SUBB, np.arange(SUBB)[None, :]
    masks = [j == col] + [(j // (2 * h) == col // (2 * h)) & (j // h % 2 == 0) & (col // h % 2 == 1) for h in LEVELS]
    arrays = {
        "xT": rows(x.reshape(NB * T, HID).T),
        "eye": np.eye(P, dtype=np.float32),
        "masks": np.stack(masks, axis=1).astype(np.float32),
        "head_w": heads,
        "out_w": out_w,
        "wfa": rows(i[A + "Wfa"]), "wga": rows(i[A + "Wga"]), "wb": rows(i[A + "Wb"]),
        "taps": conv.transpose(2, 0, 1, 3),
        "dt_bias": i[A + "dt_bias"].reshape(H, P).T,
        "a_log": np.broadcast_to(i[A + "A_log"].reshape(1, H), (P, H)),
        "norm_w": i[A + "norm_w"].reshape(P, 1),
        "w_gate": rows(i[FN + "w_gate"].T), "w_up": rows(i[FN + "w_up"].T), "w_down": rows(i[FN + "w_down"].T),
        "w_in": rows(i[B + "in_proj_w"].T), "w_x": rows(i[B + "x_proj_w"].T), "w_o": rows(i[B + "out_proj_w"].T),
        "m_norm": i[B + "norm_w"].reshape(KT, P).T,
        "m_taps": i[B + "conv_w"].reshape(DT, P, KC).transpose(1, 0, 2),
        "m_cb": i[B + "conv_b"].reshape(DT, P).T,
        "m_dtw": i[B + "dt_w"].reshape(DT, P).T,
        "m_dtb": i[B + "dt_b"].reshape(DT, P).T,
        "m_D": i[B + "D_param"].reshape(DT, P).T,
        "m_A": i[B + "A_log"].reshape(DT, P, NS).transpose(1, 0, 2),
    }
    arrays = {k: np.ascontiguousarray(v) for k, v in arrays.items()}
    nc = bacc.Bacc("TRN2", target_bir_lowering=False, num_devices=1)
    aps = {k: nc.dram_tensor("in_" + k, v.shape, mybir.dt.from_np(v.dtype), kind="ExternalInput").ap()
           for k, v in arrays.items()}
    aps["scratch"] = nc.dram_tensor("ssm_rows", (NB, NX, T), F32, kind="Internal").ap()
    out = nc.dram_tensor("out_xT", (P, KT, NB * T), F32, kind="ExternalOutput").ap()
    hybrid_block(nc, aps, out)
    r = run_bass_kernel_spmd(nc, [{"in_" + k: v for k, v in arrays.items()}], core_ids=[0])
    got = r.results[0]["out_xT"]
    return got.transpose(1, 0, 2).reshape(HID, NB, T).transpose(1, 2, 0)
```

```python
from contextlib import ExitStack

import concourse.bass as bass
from concourse import mybir

F32 = mybir.dt.float32
I32 = mybir.dt.int32
ALU = mybir.AluOpType
ACT = mybir.ActivationFunctionType
MUL, ADD, SUB = ALU.mult, ALU.add, ALU.subtract

P = 128
NB = 2
T = 1024
HID = 256
KT = HID // P
H = 16
KC = 4
HALO = KC - 1
CH = 64
SUBB = CH // 2
SEG = 512
NSEG = T // SEG
NC = SEG // CH
FF = 1024
DI = 512
DT = DI // P
NS = 16
NX = 2 * NS + 1
LEVELS = [1, 2, 4, 8, 16]
BANK = 512


class Lane:

    def __init__(self, sem, one_by_one=False):
        self.sem, self.count, self.program, self.waited = sem, 0, [], {}
        self.one_by_one = one_by_one

    def wait(self, *marks):
        need = {}
        for mark in marks:
            if isinstance(mark, list):
                for m in mark:
                    if m is not None:
                        need[m[0]] = max(need.get(m[0], 0), m[1])
            elif mark is not None:
                need[mark[0]] = max(need.get(mark[0], 0), mark[1])
        for sem, value in need.items():
            if self.waited.get(sem, 0) < value:
                self.waited[sem] = value
                self.program.append(lambda eng, sem=sem, value=value: eng.wait_ge(sem, value))

    def do(self, steps, *after):
        self.wait(*after)
        if not isinstance(steps, list):
            steps = [steps]
        if self.one_by_one:
            for step in steps[:-1]:
                self.wait((self.sem, self.count))
                self.count += 1
                self.program.append(lambda eng, step=step: step(eng).then_inc(self.sem, 1))
            self.wait((self.sem, self.count))
        else:
            self.program += steps[:-1]
        self.count += 1
        self.program.append(lambda eng, last=steps[-1]: last(eng).then_inc(self.sem, 1))
        return (self.sem, self.count)

    def play(self, eng):
        for step in self.program:
            step(eng)


def spread(ap, axis, n):
    a = ap.unsqueeze(axis)
    shape = list(a.shape)
    shape[axis] = n
    return a.broadcast_to(shape)


def braid(streams, lengths):
    live = [[name, gen, 0] for name, gen in streams]
    while live:
        item = min(live, key=lambda it: it[2] / lengths.get(it[0], 50))
        try:
            next(item[1])
            item[2] += 1
        except StopIteration:
            lengths[item[0]] = max(item[2], 1)
            live.remove(item)


def hybrid_block(nc, a, out):
    ctx = ExitStack()
    with ctx:
        def sb(name, shape, dt=F32, scope=ctx):
            return scope.enter_context(nc.sbuf_tensor(name, shape, dt))

        def sem(name):
            return ctx.enter_context(nc.semaphore(name))

        pe, dve, act, pool, sp = (Lane(sem("done_" + n), n == "gpsimd")
                                  for n in ("tensor", "vector", "scalar", "gpsimd", "sync"))
        psum = [ctx.enter_context(nc.psum_tensor(f"bank{i}", [P, BANK], F32)) for i in range(8)]
        bank_free = [None] * 8

        dma_total = {}

        def load(queue, name, pairs, *after):
            if name not in dma_total:
                dma_total[name] = [sem("dma_" + name), 0]
            entry = dma_total[name]
            queue.wait(*after)
            for dst, src in pairs:
                entry[1] += 16
                queue.program.append(lambda eng, d=dst, s=src, q=entry[0]: eng.dma_start(d, s).then_inc(q, 16))
            return (entry[0], entry[1])

        xT = sb("xT", [P, KT, NB * T])
        mean_w = sb("mean_w", [P, P])
        ones = sb("ones", [P, P])
        eye = sb("eye", [P, P])
        biases = sb("biases", [P, 4])
        cen = sb("cen", [P, KT, SEG])
        sq = sb("sq", [P, KT, SEG])

        loaded_x = load(sp, "x", [(xT[:, :, :], a["xT"])])
        loaded_eye = load(sp, "eye", [(eye[:, :], a["eye"])])
        const_ready = pool.do([lambda e: e.memset(mean_w[:, :], 1.0 / HID),
                               lambda e: e.memset(ones[:, :], 1.0),
                               lambda e: e.memset(biases[:, 0:1], 1e-5),
                               lambda e: e.memset(biases[:, 1:2], 1e-6),
                               lambda e: e.memset(biases[:, 2:3], 1.0),
                               lambda e: e.memset(biases[:, 3:4], P * 1e-6)])
        EPS5, EPS6, ONE, EPSQ = (biases[:, i:i + 1] for i in range(4))

        def mm(bank_ap, lhsT, rhs, start=True, stop=True, loose=False):
            return lambda e: e.matmul(bank_ap, lhsT, rhs, start=start, stop=stop, skip_group_check=loose)

        def tt(o, x, y, op):
            return lambda e: e.tensor_tensor(o, x, y, op)

        def fn(o, i, f, **kw):
            return lambda e: e.activation(o, i, f, **kw)

        def table_set(name):
            act.program.append(lambda e: e.preload_act_table_set(name))

        LN_EXP, SILU_TANH = "natural_log_exp_and_others", "silu_and_others"
        norm_free = [None, None]

        def normalise(src, dst, banks, center, ready, dst_free, rstd, weight=None):
            b0, b1 = banks
            if center:
                summed = pe.do([mm(psum[b0][:, :], mean_w[:, :], src[:, k, :], k == 0, k == KT - 1)
                                for k in range(KT)], ready, const_ready, bank_free[b0])
                yield
                centred = dve.do(tt(cen[:, :, :], src, spread(psum[b0][:, :], 1, KT), SUB), summed, norm_free[0])
                bank_free[b0] = centred
                base = cen[:, :, :]
            else:
                centred, base = ready, src
            yield
            squared = act.do(fn(sq[:, :, :], base, ACT.Square), centred, norm_free[1])
            yield
            varied = pe.do([mm(psum[b1][:, :], mean_w[:, :], sq[:, k, :], k == 0, k == KT - 1)
                            for k in range(KT)], squared, const_ready, bank_free[b1])
            norm_free[1] = varied
            yield
            logged = act.do(fn(rstd, psum[b1][:, :], ACT.Ln, bias=EPS5), varied, norm_free[0])
            bank_free[b1] = logged
            inv = act.do(fn(rstd, rstd, ACT.Exp, scale=-0.5), logged)
            yield
            if weight is None:
                done = dve.do(tt(dst, base, spread(rstd, 1, KT), MUL), inv, dst_free)
            else:
                done = dve.do([lambda e, k=k: e.scalar_tensor_tensor(
                    dst[:, k, :], base[:, k, :], weight[:, k:k + 1], rstd, MUL, MUL)
                    for k in range(KT)], inv, dst_free)
            norm_free[0] = done
            normalise.done = done
            yield

        with ExitStack() as att:
            def sa(name, shape, dt=F32):
                return sb(name, shape, dt, att)

            xn = sa("xn", [P, KT, NB, T])
            hfa = sa("hfa", [P, 2, SEG])
            hga = sa("hga", [P, 2, SEG])
            wfa = sa("wfa", [P, KT, P])
            wga = sa("wga", [P, KT, P])
            wb = sa("wb", [P, KT, H])
            masks = sa("masks", [P, 6, SUBB])
            taps = sa("taps", [P, H, 3, KC])
            dt_bias = sa("dt_bias", [P, H])
            neg_a = sa("neg_a", [P, H])
            norm_w = sa("norm_w", [P, 1])
            beta = sa("beta", [P, T // CH, H])
            tails = sa("tails", [P, H, 3, NB, HALO])
            W = [sa(f"W{i}", [P, 7 * P]) for i in range(2)]
            WO = [sa(f"WO{i}", [P, P + HID]) for i in range(2)]
            raw = [sa(f"raw{i}", [P, NB, HALO + SEG]) for i in range(2)]
            vc = sa("vc", [P, NC, NB, CH])
            tmp, tmp2 = cen, sq
            qn = [sa(f"qn{i}", [P, NC, NB, CH]) for i in range(2)]
            kL = [sa(f"kL{i}", [P, NC, NB, CH]) for i in range(2)]
            gate = [sa(f"gate{i}", [P, NC, NB, CH]) for i in range(2)]
            R = [sa(f"R{i}", [P, 2, NC, NB, CH]) for i in range(2)]
            vT = [sa(f"vT{i}", [P, NC, P]) for i in range(3)]
            kRT = sa("kRT", [P, NC, P])
            WT = [sa(f"WT{i}", [P, NC, P]) for i in range(2)]
            kT = [sa(f"kT{i}", [P, NC, P]) for i in range(2)]
            tot = {2 * h: sa(f"tot{2 * h}", [P, NB * SEG // (2 * h)]) for h in LEVELS}
            tot_chunk = [sa(f"tot_chunk{i}", [P, NC, NB]) for i in range(2)]
            Bd = sa("Bd", [P, NC, P])
            Xd = sa("Xd", [P, NC, P])
            Bt = sa("Bt", [P, NC, P])
            Xfull = sa("Xfull", [P, NC, P])
            Bc = sa("Bc", [P, NC, SUBB])
            Xc = sa("Xc", [P, NC, SUBB])
            X = sa("X", [P, NC, SUBB])
            bs = [sa(f"bs{i}", [P, NC]) for i in range(2)]
            knorm = sa("knorm", [P, 2, NC])
            Oc = sa("Oc", [P, NC, SUBB])
            bm = sa("bm", [P, NC, SUBB])
            Ac = sa("Ac", [P, NC, SUBB])
            AT = [sa(f"AT{i}", [P, NC, CH]) for i in range(2)]
            S = sa("S", [P, H, NB, P])
            Sx = sa("Sx", [P, NB, P])
            dpad = [sa(f"dpad{i}", [P, NB, P]) for i in range(2)]
            oT = sa("oT", [P, NC, NB, CH])

            PROJ = (0, 1, 5)
            PROD, INV, CHAIN = 2, 3, 4
            OUT = (6, 7)
            turn = [0]

            def flat(t):
                return t[:, :, :, :].rearrange("p c b t -> p (c b t)")

            def halves(t):
                return flat(t).rearrange("p (a n) -> p a n", a=2)

            def pair_cols(t, c):
                return t[:, c, :, :].rearrange("p b t -> p (b t)")

            def half_cols(t, seg, a):
                base = seg * SEG + a * 4 * CH
                return t[:, :, base:base + 4 * CH].rearrange("p b (c t) -> p c b t", t=CH)

            def proj_bank():
                turn[0] += 1
                return PROJ[turn[0] % len(PROJ)]

            small = load(sp, "small", [(wfa[:, :, :], a["wfa"]), (wga[:, :, :], a["wga"]), (wb[:, :, :], a["wb"]),
                                       (masks[:, :, :], a["masks"]), (taps[:, :, :, :], a["taps"]),
                                       (dt_bias[:, :], a["dt_bias"]), (neg_a[:, :], a["a_log"]),
                                       (norm_w[:, :], a["norm_w"])])
            w_loaded, wo_loaded, w_free, wo_free = {}, {}, [None, None], [None, None]

            def load_head(g):
                h = g % H
                w_loaded[g] = load(sp, f"w{g % 2}", [(W[g % 2][:, :], a["head_w"][h])], w_free[g % 2])

            load_head(0)

            zeroed = pool.do([lambda e, t=t: e.memset(t[:, :, :], 0.0)
                              for t in [Bd, Xd, Bt, Xfull, AT[0], AT[1], dpad[0], dpad[1]]])
            bank_zeroed = dve.do(lambda e: e.memset(psum[PROD][:, :], 0.0))
            bank_free[PROD] = bank_zeroed
            s_zeroed = dve.do(lambda e: e.memset(S[:, :, :, :], 0.0))
            expa = act.do(fn(neg_a[:, :], neg_a[:, :], ACT.Exp), small)
            table_set(LN_EXP)
            a_ready = dve.do(lambda e: e.tensor_scalar(neg_a[:, :], neg_a[:, :], -1.0, None, MUL), expa)

            nw_ready = dve.do(lambda e: e.tensor_scalar(norm_w[:, :], norm_w[:, :], 0.5, None, MUL), small)
            xn_ready = []
            xflat = xn[:, :, :, :].rearrange("p k b t -> p k (b t)")
            for n in range(NB * T // SEG):
                cols = slice(n * SEG, (n + 1) * SEG)
                for _ in normalise(xT[:, :, cols], xflat[:, :, cols],
                                   (2 * (n % 2), 2 * (n % 2) + 1), True, loaded_x, None,
                                   vc[:, 0:NC // NB, :, :].rearrange("p c b t -> p (c b t)")):
                    pass
                xn_ready.append(normalise.done)
            logits = pe.do([mm(psum[0][b * CH:(b + 1) * CH, c * H:(c + 1) * H], xn[:, k, b, c * CH:(c + 1) * CH],
                               wb[:, k, :], k == 0, k == KT - 1)
                            for c in range(T // CH) for b in range(NB) for k in range(KT)],
                           xn_ready, small, bank_free[0])
            beta_ready = act.do(fn(beta[:, :, :].rearrange("p c h -> p (c h)"), psum[0][:, 0:T // CH * H],
                                   ACT.Sigmoid), logits)
            bank_free[0] = beta_ready

            def low_rank(w, dst, seg, dst_free):
                marks = []
                for a2 in range(2):
                    bank = proj_bank()
                    m = pe.do([mm(psum[bank][:, :], w[:, k, :], half_cols(xn[:, k, :, :], seg, a2), k == 0,
                                  k == KT - 1) for k in range(KT)], xn_ready, small, bank_free[bank])
                    bank_free[bank] = act.do(fn(dst[:, a2, :], psum[bank][:, :], ACT.Copy), m, dst_free)
                    marks.append(bank_free[bank])
                return marks

            hfa_ready, hga_ready, hfa_read, hga_read = {}, {}, [None], [None]

            front_done, tree_done, state_done = {}, {}, {}
            raw_free = [None, None]
            last = {"knorm": None, "xc_read": None, "bc_read": None, "tree": None, "oT": None, "small": None}
            last["tmp"] = last["tmp2"] = last["vc"] = list(norm_free)

            def front(g):
                seg, h = divmod(g, H)
                s = g % 2
                if g + 1 < NSEG * H:
                    load_head(g + 1)
                w = W[s]
                if h == 0:
                    hfa_ready[seg] = low_rank(wfa, hfa, seg, hfa_read[0])
                cols = slice(seg * SEG, (seg + 1) * SEG)
                dsts = (qn[s], kL[s], vc)
                silued = [None] * 3
                slot_free = tree_done.get(g - 2, None)
                absd, relud = [], []

                def gate_product(b):
                    bank = proj_bank()
                    m = hfa_read[0] = pe.do(mm(psum[bank][:, :], w[:, 6 * P:7 * P], hfa[:, b, :]), w_loaded[g],
                                            hfa_ready[seg], bank_free[bank])
                    absd.append(act.do(fn(tmp2[:, b, :], psum[bank][:, :], ACT.Abs, bias=dt_bias[:, h:h + 1]), m,
                                       small, last["tmp2"]))
                    relud.append(dve.do(lambda e: e.tensor_scalar(
                        halves(gate[s])[:, b, :], psum[bank][:, :], dt_bias[:, h:h + 1], 0.0, ADD, ALU.max),
                        absd[-1], slot_free))
                    bank_free[bank] = relud[-1]

                halos, evacs = {}, {}

                def tap(kind, i):
                    return taps[:, h, kind, i:i + 1]

                def conv_out(kind):
                    return dsts[kind][:, :, :, :].rearrange("p c b t -> p b c t")

                def halo(kind):
                    rb = (3 * g + kind) % 2
                    if seg == 0:
                        halos[kind] = pool.do(lambda e: e.memset(raw[rb][:, :, 0:HALO], 0.0), raw_free[rb])
                    else:
                        halos[kind] = pool.do(lambda e: e.tensor_copy(raw[rb][:, :, 0:HALO], tails[:, h, kind, :, :]),
                                              raw_free[rb])
                    evacs[kind] = []

                def project(kind, b):
                    rb = (3 * g + kind) % 2
                    bank = proj_bank()
                    m = w_free[s] = pe.do([mm(psum[bank][:, :], w[:, (kind * KT + k) * P:(kind * KT + k + 1) * P],
                                              xn[:, k, b, cols], k == 0, k == KT - 1) for k in range(KT)],
                                          w_loaded[g], xn_ready, bank_free[bank])
                    copied = act.do(fn(raw[rb][:, b, HALO:], psum[bank][:, :], ACT.Copy), m, raw_free[rb])
                    bank_free[bank] = act.do(fn(conv_out(kind)[:, b, :, :],
                                                psum[bank][:, :].rearrange("p (c t) -> p c t", t=CH), ACT.Copy,
                                                scale=tap(kind, KC - 1)), small,
                                             last["vc"] if kind == 2 else slot_free)
                    evacs[kind] += [copied, bank_free[bank]]

                halo(0)
                for b in range(NB):
                    project(0, b)
                    yield
                for kind in range(3):
                    rb = (3 * g + kind) % 2
                    kept = None
                    if seg == 0:
                        kept = pool.do(lambda e, rb=rb, kind=kind: e.tensor_copy(
                            tails[:, h, kind, :, :], raw[rb][:, :, SEG:SEG + HALO]), evacs[kind])
                    if kind < 2:
                        halo(kind + 1)
                    m = evacs[kind]
                    for i in range(KC - 1):
                        if kind == 2 and i == 0:
                            squared = act.do(fn(tmp[:, :, :], halves(kL[s]), ACT.Square), silued[1], last["tmp"])
                        if kind == 2 and i == KC - 2:
                            bank = proj_bank()
                            tsq = tmp[:, :, :].rearrange("p a (c n) -> p (a c) n", n=P)
                            last["tmp"] = pe.do([mm(psum[bank][:, c:c + 1], tsq[:, c, :], ones[:, 0:1])
                                                 for c in range(NC)], squared, const_ready, bank_free[bank])
                            k_summed = bank_free[bank] = act.do(fn(knorm[:, 0, :], psum[bank][:, 0:NC], ACT.Copy),
                                                                last["tmp"], last["knorm"])
                        m = dve.do([lambda e, rb=rb, kind=kind, i=i, b=b: e.scalar_tensor_tensor(
                            conv_out(kind)[:, b, :, :], raw[rb][:, b, i:i + SEG].rearrange("p (c t) -> p c t", t=CH),
                            tap(kind, i), conv_out(kind)[:, b, :, :], MUL, ADD) for b in range(NB)],
                            m, halos[kind], small)
                        if i < NB:
                            if kind < 2:
                                project(kind + 1, i)
                            else:
                                gate_product(i)
                        yield
                    w_free[s] = hfa_read[0]
                    raw_free[rb] = [m, kept]
                    if kind == 0:
                        table_set(SILU_TANH)
                    silued[kind] = act.do(fn(dsts[kind][:, :, :, :], dsts[kind][:, :, :, :], ACT.Silu), m)
                    yield
                table_set(LN_EXP)
                m = act.do(fn(knorm[:, 0, :], knorm[:, 0, :], ACT.Ln, bias=EPS6), k_summed)
                inv2 = act.do(fn(bs[s][:, :], knorm[:, 0, :], ACT.Exp, scale=-1.0), m, slot_free)
                norm_k = act.do(fn(knorm[:, 1, :], knorm[:, 0, :], ACT.Exp, scale=0.5), m)
                bs_ready = dve.do(tt(bs[s][:, :], bs[s][:, :], beta[:, seg * NC:(seg + 1) * NC, h], MUL), inv2,
                                  beta_ready)
                m = act.do(fn(tmp2[:, :, :], tmp2[:, :, :], ACT.Exp, scale=-1.0), absd)
                m = act.do(fn(tmp2[:, :, :], tmp2[:, :, :], ACT.Ln, bias=ONE), m)
                yield
                m = dve.do(tt(halves(gate[s]), halves(gate[s]), tmp2[:, :, :], ADD), m, relud)
                last["tmp2"] = m
                gated = act.do(fn(flat(gate[s]), flat(gate[s]), ACT.Exp, scale=neg_a[:, h:h + 1]), m, a_ready)
                vt_free = state_done.get(g - 3, None)
                turned = []
                for half in range(2):
                    bank = proj_bank()
                    m = pe.do([lambda e, c=c, bank=bank: e.transpose(
                        psum[bank][:, (c % 4) * P:(c % 4 + 1) * P], pair_cols(vc, c), eye[:, :])
                        for c in range(4 * half, 4 * half + 4)], silued[2], loaded_eye, bank_free[bank])
                    last["vc"] = m
                    turned.append(dve.do(tt(vT[g % 3][:, 4 * half:4 * half + 4, :],
                                            psum[bank][:, :].rearrange("p (c d) -> p c d", c=4),
                                            spread(knorm[:, 1, 4 * half:4 * half + 4], 2, P), MUL),
                                         m, norm_k, vt_free))
                    bank_free[bank] = turned[-1]
                    yield
                last["knorm"] = turned[-1]
                t = halves(qn[s])
                squared = act.do(fn(tmp[:, :, :], t, ACT.Square), silued[0], last["tmp"])
                yield
                logs = []
                for b in range(NB):
                    bank = proj_bank()
                    m = pe.do(mm(psum[bank][:, :], ones[:, :], tmp[:, b, :]), squared, const_ready, bank_free[bank])
                    last["tmp"] = m
                    logs.append(act.do(fn(tmp2[:, b, :], psum[bank][:, :], ACT.Ln, bias=EPSQ, scale=float(P)), m,
                                       last["tmp2"]))
                    bank_free[bank] = logs[-1]
                    yield
                inv = act.do(fn(tmp2[:, :, :], tmp2[:, :, :], ACT.Exp, scale=-0.5), logs)
                m = pool.do(tt(t, t, tmp2[:, :, :], MUL), inv)
                last["tmp2"] = m
                normed = [m, silued[1], bs_ready]
                yield
                front_done[g] = normed + turned + [gated]
                yield

            def tree(g):
                seg, h = divmod(g, H)
                s = g % 2
                ready = front_done[g]
                r_free = state_done.get(g - 2, None)
                wo_loaded[g] = load(sp, f"wo{s}", [(WO[s][:, :], a["out_w"][h])], wo_free[s])
                Rf = R[s][:, :, :, :, :].rearrange("p a c b t -> p a (c b t)")
                Lf = flat(kL[s])
                beta_g = bs[s][:, :]
                bank = PROD

                def quad(w):
                    return slice(SUBB * w, SUBB * (w + 1))

                def block(t, c, b, u):
                    return t[:, c, b, u * SUBB:(u + 1) * SUBB]

                def block_r(c, b, u):
                    return R[s][:, :, c, b, u * SUBB:(u + 1) * SUBB]

                def product(half, r_ready, l_ready):
                    steps = []
                    for c in range(NC):
                        for w in range(4):
                            b, u = w // 2, w % 2
                            o, r = psum[bank][quad(w), c * CH:(c + 1) * CH], block_r(c, b, u)
                            if half > 1:
                                o = o.rearrange("p (a n two t) -> p a n two t", a=2, two=2, t=half)[:, :, :, 1, :]
                                r = r.rearrange("p a (n two t) -> p a n two t", two=2, t=half)[:, :, :, 1, :]
                            else:
                                o = o.rearrange("p (a i) -> p a i", a=2)
                            steps.append(mm(o, block(kL[s], c, b, u), r))
                    return pe.do(steps, r_ready, l_ready, bank_free[bank])

                view = psum[bank][:, :].rearrange("p (c a i) -> p c a i", c=NC, a=2)
                inv_x = psum[INV][:, 0:NC * SUBB].rearrange("p (c i) -> p c i", c=NC)

                def mask(li):
                    return spread(masks[:, li, :], 1, NC)

                def blocks(lhsT, rhs, *after):
                    return pe.do([mm(psum[INV][quad(w), c * SUBB:(c + 1) * SUBB], lhsT[:, c, quad(w)], rhs(c))
                                  for c in range(NC) for w in range(4)], *after)

                def on_diagonal(dst, src, *after):
                    return act.do([fn(dst[quad(w), :, quad(w)], src[quad(w), :, :], ACT.Copy) for w in range(4)],
                                  zeroed, *after)

                def x_transposed(dst, x_made, dst_free):
                    m = dve.do(lambda e: e.transpose(Xc[:, :, :].rearrange("p c i -> p (c i)"),
                                                     X[:, :, :].rearrange("p c i -> p (c i)")),
                               x_made, last["xc_read"])
                    last["xc_read"] = on_diagonal(dst, Xc, m, dst_free)
                    return last["xc_read"]

                prod = pe.do([mm(psum[bank][quad(2 * b + u), c * SUBB:(c + 1) * SUBB], block(kL[s], c, b, u),
                                 block(qn[s], c, b, u)) for c in range(NC) for b in range(NB) for u in range(2)],
                             ready, bank_free[bank])
                rk = dve.do(tt(Rf[:, 0, :], Lf, flat(gate[s]), MUL), ready, r_free)
                rq = pool.do(tt(Rf[:, 1, :], flat(qn[s]), flat(gate[s]), MUL), ready, r_free)
                acc = dve.do(tt(Ac[:, :, :], psum[bank][:, 0:NC * SUBB].rearrange("p (c i) -> p c i", c=NC),
                                mask(0), MUL), prod, small, last["tree"])
                bank_free[bank] = acc
                r_ready, l_ready = [rk, rq], ready
                t_ready, t_now = ready, flat(gate[s])
                tree_free = last["tree"]
                yield
                p1 = oc = xs = xd = bm_free = None
                x_free = bd_free = tree_free

                def x_step(x_free):
                    p2 = blocks(Xd, lambda c: Oc[:, c, :], oc, xd)
                    xs = dve.do(tt(X[:, :, :], X[:, :, :], inv_x, SUB), p2)
                    bank_free[INV] = xs
                    return p2, xs

                for li, half in enumerate(LEVELS):
                    prod = product(half, r_ready, l_ready)
                    bmd = pool.do(tt(bm[:, :, :], mask(1 + li), spread(beta_g, 2, SUBB), MUL),
                                  ready, small, bm_free, last["small"])
                    yield
                    pair = t_now.rearrange("p (n two) -> p n two", two=2)
                    Rv = Rf.rearrange("p a (n two t) -> p a n two t", two=2, t=half)
                    Lv = Lf.rearrange("p (n two t) -> p n two t", two=2, t=half)
                    up_t = (pool if half > 1 else dve).do(
                        tt(tot[2 * half][:, :], pair[:, :, 0], pair[:, :, 1], MUL), t_ready, tree_free)
                    up_q = pool.do(tt(Rv[:, 1, :, 1, :], Rv[:, 1, :, 1, :], spread(pair[:, :, 0], 2, half), MUL),
                                   prod, t_ready)
                    if half > 2:
                        p2, xs = x_step(x_free)
                        x_free = p2
                    up_k = dve.do(tt(Rv[:, 0, :, 1, :], Rv[:, 0, :, 1, :], spread(pair[:, :, 0], 2, half), MUL),
                                  prod, t_ready)
                    up_l = (pool if half > 1 else dve).do(
                        tt(Lv[:, :, 0, :], Lv[:, :, 0, :], spread(pair[:, :, 1], 2, half), MUL), prod, t_ready)
                    r_ready, l_ready, t_ready, t_now = [up_q, up_k], up_l, up_t, tot[2 * half][:, :]
                    yield
                    bm_free = dve.do(tt(Bc[:, :, :], view[:, :, 0, :], bm[:, :, :], MUL), prod, bmd,
                                     last["bc_read"])
                    bd = last["bc_read"] = on_diagonal(Bd, Bc, bm_free, bd_free)
                    yield
                    acc = dve.do(lambda e, li=li: e.copy_predicated(
                        Ac[:, :, :], mask(1 + li).bitcast(I32), view[:, :, 1, :]), acc, prod)
                    bank_free[bank] = acc
                    last["small"] = bm_free
                    yield
                    rhs = (lambda c: masks[:, 0, :]) if half == 1 else (lambda c: X[:, c, :])
                    p1 = blocks(Bd, rhs, bd, xs, bank_free[INV])
                    bd_free = p1
                    if half > 1:
                        xd = x_transposed(Xd, xs, x_free)
                    if half == 1:
                        xs = dve.do(tt(X[:, :, :], mask(0), inv_x, SUB), p1, x_free)
                        bank_free[INV] = xs
                    else:
                        oc = act.do(fn(Oc[:, :, :], inv_x, ACT.Copy), p1, x_free)
                    yield
                prod = pe.do([mm(psum[bank][quad(2 * b), c * CH:(c + 1) * CH], block(kL[s], c, b, 0),
                                 block_r(c, b, 1)) for c in range(NC) for b in range(NB)],
                             r_ready, l_ready, bank_free[bank])
                p2, xs = x_step(x_free)
                pair = t_now.rearrange("p (n two) -> p n two", two=2)
                Rv = Rf.rearrange("p a (n two t) -> p a n two t", two=2, t=SUBB)
                Lv = Lf.rearrange("p (n two t) -> p n two t", two=2, t=SUBB)
                up_q = pool.do(tt(Rv[:, 1, :, 1, :], Rv[:, 1, :, 1, :], spread(pair[:, :, 0], 2, SUBB), MUL),
                               prod, t_ready)
                up_l = pool.do(tt(Lv[:, :, 0, :], Lv[:, :, 0, :], spread(pair[:, :, 1], 2, SUBB), MUL), prod, t_ready)
                up_t = pool.do(tt(tot_chunk[s][:, :, :].rearrange("p c b -> p (c b)"), pair[:, :, 0], pair[:, :, 1],
                                  MUL), t_ready, r_free)
                scaled = pool.do(tt(Ac[:, :, :], Ac[:, :, :], spread(beta_g, 2, SUBB), MUL), acc)
                bt = dve.do([tt(Bt[quad(w), :, quad(w + 1)], view[quad(w), :, 0, :],
                                spread(beta_g[quad(w), :], 2, SUBB), MUL) for w in (0, 2)], prod, zeroed, tree_free)
                yield
                p1 = blocks(Bt, lambda c: X[:, c, :], bt, xs, bank_free[INV])
                xd = x_transposed(Xfull, xs, tree_free)
                up_k = dve.do(tt(Rv[:, 0, :, 1, :], Rv[:, 0, :, 1, :], spread(pair[:, :, 0], 2, SUBB), MUL),
                              prod, t_ready)
                at = dve.do([tt(AT[s][quad(w), :, SUBB:CH], view[quad(w), :, 1, :],
                                spread(beta_g[quad(w), :], 2, SUBB), MUL) for w in (0, 2)], zeroed, r_free)
                bank_free[bank] = at
                oc = act.do(lambda e: e.activation(Oc[:, :, :], inv_x, ACT.Copy, scale=-1.0), p1, p2)
                yield
                p2 = blocks(Xfull, lambda c: Oc[:, c, :], oc, xd)
                low = act.do([lambda e, w=w: e.activation(
                    AT[s][quad(w), :, SUBB * (w % 2):SUBB * (w % 2 + 1)], Ac[quad(w), :, :], ACT.Copy)
                    for w in range(4)], scaled, zeroed, r_free)
                yield
                xc_ = dve.do(lambda e: e.tensor_copy(X[:, :, :], inv_x), p2)
                bank_free[INV] = xc_
                xf = dve.do([lambda e, w=w: e.transpose(Xfull[quad(w - 1), :, quad(w)], X[quad(w), :, :])
                             for w in (1, 3)], xc_)
                yield
                turned = []
                for q in range(2):
                    b2 = proj_bank()
                    m = pe.do([lambda e, c=c, b2=b2: e.transpose(
                        psum[b2][:, (c % 4) * P:(c % 4 + 1) * P],
                        R[s][:, 0, c, :, :].rearrange("p b t -> p (b t)"), eye[:, :])
                        for c in range(4 * q, 4 * q + 4)], up_k, loaded_eye, bank_free[b2])
                    turned.append(act.do(fn(kRT[:, 4 * q:4 * q + 4, :].rearrange("p c d -> p (c d)"),
                                            psum[b2][:, :], ACT.Copy), m, tree_free))
                    bank_free[b2] = turned[-1]
                yield
                keyed = []
                for q in range(2):
                    b2 = proj_bank()
                    m = pe.do([lambda e, c=c, b2=b2: e.transpose(
                        psum[b2][:, (c % 4) * P:(c % 4 + 1) * P], pair_cols(kL[s], c), eye[:, :])
                        for c in range(4 * q, 4 * q + 4)], up_l, bank_free[b2])
                    keyed.append(dve.do(tt(kT[s][:, 4 * q:4 * q + 4, :],
                                           psum[b2][:, :].rearrange("p (c d) -> p c d", c=4),
                                           spread(beta_g[:, 4 * q:4 * q + 4], 2, P), MUL), m, r_free))
                    bank_free[b2] = keyed[-1]
                yield
                solved = []
                for q in range(2):
                    b2 = proj_bank()
                    m = pe.do([mm(psum[b2][:, (c % 4) * P:(c % 4 + 1) * P], Xfull[:, c, :], vT[g % 3][:, c, :])
                               for c in range(4 * q, 4 * q + 4)], xf, xd, ready, bank_free[b2])
                    solved.append(act.do(fn(vT[g % 3][:, 4 * q:4 * q + 4, :].rearrange("p c d -> p (c d)"),
                                            psum[b2][:, :], ACT.Copy), m))
                    bank_free[b2] = solved[-1]
                    b2 = proj_bank()
                    m = pe.do([mm(psum[b2][:, (c % 4) * P:(c % 4 + 1) * P], kRT[:, c, :], Xfull[:, c, :])
                               for c in range(4 * q, 4 * q + 4)], turned, bank_free[b2])
                    solved.append(act.do(fn(WT[s][:, 4 * q:4 * q + 4, :].rearrange("p c d -> p (c d)"),
                                            psum[b2][:, :], ACT.Copy), m, r_free))
                    bank_free[b2] = solved[-1]
                    yield
                last["tree"] = [xf, at, low, xd, p2, up_t, m]
                tree_done[g] = [up_q, up_k, up_t, low, at, xf, m] + keyed + solved
                yield

            s_ready = {h: [s_zeroed, s_zeroed] for h in range(H)}
            dpad_free = [None, None]
            chain = {"sx": None}
            x_added = [None] * (NB * NSEG)

            def state(g):
                seg, h = divmod(g, H)
                s = g % 2
                ready = tree_done[g]
                upd = s_ready[h]
                o_evac = []
                if h == 0:
                    hga_ready[seg] = low_rank(wga, hga, seg, hga_read[0])
                tanh_g = R[s][:, 0, :, :, :].rearrange("p c b t -> p (c b t)").rearrange("p (a n) -> p a n", a=2)
                for c in range(NC):
                    if c == 3:
                        table_set(SILU_TANH)
                        tanhed = []
                        for a2 in range(2):
                            bank = proj_bank()
                            hga_read[0] = pe.do(mm(psum[bank][:, :], WO[s][:, 0:P], hga[:, a2, :]), wo_loaded[g],
                                                hga_ready[seg], bank_free[bank])
                            tanhed.append(act.do(fn(tanh_g[:, a2, :], psum[bank][:, :], ACT.Tanh, scale=0.5), hga_read[0],
                                                 ready))
                            bank_free[bank] = tanhed[-1]
                    src = S[:, h, :, :] if c % 2 == 0 else Sx[:, :, :]
                    dst = Sx[:, :, :] if c % 2 == 0 else S[:, h, :, :]
                    d = dpad[c % 2]
                    ob = OUT[c // 4]
                    ocol = lambda b, c=c: slice((c % 4) * P + b * CH, (c % 4) * P + (b + 1) * CH)
                    pred = pe.do([mm(psum[CHAIN][b * CH:(b + 1) * CH, 0:P], WT[s][:, c, b * CH:(b + 1) * CH],
                                     src[:, b, :]) for b in range(NB)], ready, upd, bank_free[CHAIN])
                    seen = pe.do([mm(psum[ob][:, ocol(b)], src[:, b, :], R[s][:, 1, c, b, :],
                                     start=(c % 4 == 0 and b == 0), stop=False, loose=True) for b in range(NB)],
                                 bank_free[ob])
                    dd = dve.do([tt(d[b * CH:(b + 1) * CH, b, :], vT[g % 3][b * CH:(b + 1) * CH, c, :],
                                    psum[CHAIN][b * CH:(b + 1) * CH, 0:P], SUB) for b in range(NB)],
                                pred, ready, zeroed, dpad_free[c % 2])
                    bank_free[CHAIN] = dd
                    yield
                    outer = pe.do(mm(psum[CHAIN][:, P:(1 + NB) * P], kT[s][:, c, :], d[:, :, :].rearrange("p b v -> p (b v)")),
                                  dd)
                    within = pe.do([mm(psum[ob][:, ocol(b)], d[:, b, :], AT[s][:, c, :], start=False, stop=True,
                                       loose=True) for b in range(NB)])
                    upd = dve.do([lambda e, b=b, src=src, dst=dst, c=c: e.scalar_tensor_tensor(
                        dst[:, b, :], src[:, b, :], tot_chunk[s][:, c, b:b + 1], psum[CHAIN][:, (1 + b) * P:(2 + b) * P],
                        MUL, ADD) for b in range(NB)], outer, seen)
                    bank_free[CHAIN] = upd
                    dpad_free[c % 2] = within
                    if c % 4 == 3:
                        k = c // 4
                        m = act.do(fn(halves(oT)[:, k, :], psum[ob][:, :], ACT.Copy), within, last["oT"])
                        bank_free[ob] = m
                        o_evac.append(m)
                    yield
                s_ready[h] = upd
                tmp3 = WT[s][:, :, :].rearrange("p c d -> p (c d)").rearrange("p (a n) -> p a n", a=2)
                tmp4 = R[s][:, 1, :, :, :].rearrange("p c b t -> p (c b t)").rearrange("p (a n) -> p a n", a=2)
                oh = halves(oT)
                table_set(LN_EXP)
                squared = act.do(fn(tmp3, oh, ACT.Square), o_evac, within)
                yield
                logs = []
                for b in range(NB):
                    bank = proj_bank()
                    m = pe.do(mm(psum[bank][:, :], ones[:, :], tmp3[:, b, :]), squared, bank_free[bank])
                    logs.append(act.do(fn(tmp4[:, b, :], psum[bank][:, :], ACT.Ln, bias=EPS6, scale=1.0 / P), m,
                                       within))
                    bank_free[bank] = logs[-1]
                inv = act.do(fn(tmp4, tmp4, ACT.Exp, scale=-0.5), logs)
                yield
                m = dve.do(lambda e: e.scalar_tensor_tensor(tmp4, tanh_g, 1.0, tmp4, ADD, MUL), inv, tanhed)
                m = dve.do(lambda e: e.scalar_tensor_tensor(oh, oh, norm_w[:, 0:1], tmp4, MUL, MUL), m, nw_ready)
                scratch_read = gated = m
                yield
                for b in range(NB):
                    for k in range(KT):
                        bank = proj_bank()
                        m = pe.do(mm(psum[bank][:, :], WO[s][:, (k + 1) * P:(k + 2) * P], oh[:, b, :]), gated,
                                  bank_free[bank])
                        dst = half_cols(xT[:, k, :].rearrange("p (b t) -> p b t", b=NB), seg, b)
                        bank_free[bank] = dve.do(tt(dst, dst, psum[bank][:, :].rearrange(
                            "p (c b t) -> p c b t", b=NB, t=CH), ADD), m, chain.get((b, k)))
                        chain[(b, k)] = bank_free[bank]
                        x_added[seg] = x_added[NSEG + seg] = bank_free[bank]
                    yield
                last["oT"] = m
                wo_free[s] = m
                state_done[g] = [upd, within, scratch_read]

            lengths = {}
            NG = NSEG * H
            for step in range(NG + 2):
                streams = []
                if step >= 2:
                    streams.append(("state", state(step - 2)))
                if 1 <= step <= NG:
                    streams.append(("tree", tree(step - 1)))
                if step < NG:
                    streams.append(("front", front(step)))
                braid(streams, lengths)

        def fence():
            marks = [(lane.sem, lane.count) for lane in (pe, dve, act, pool) if lane.count]
            for lane in (pe, dve, act, pool, sp):
                lane.wait(marks)
            return marks

        def swiglu(tag, x_ready):
            with ExitStack() as ff:
                wg = sb("wg" + tag, [P, KT, FF], F32, ff)
                wu = sb("wu" + tag, [P, KT, FF], F32, ff)
                wd = sb("wd" + tag, [P, FF // P, HID], F32, ff)
                xh = [sb(f"xh{i}" + tag, [P, KT, SEG], F32, ff) for i in range(2)]
                hid = [sb(f"hid{i}" + tag, [P, FF // P, SEG], F32, ff) for i in range(2)]
                rstd = sb("rstd" + tag, [P, SEG], F32, ff)
                sg = [sb(f"sg{i}" + tag, [P, SEG], F32, ff) for i in range(2)]
                w = load(sp, "ffn" + tag, [(wg[:, :, :], a["w_gate"]), (wu[:, :, :], a["w_up"]),
                                           (wd[:, :, :], a["w_down"])])
                xh_free, hid_free, sg_free = [None] * 2, [None] * 2, [None] * 2
                added, hdone = [], {}
                tiles = NB * T // SEG

                def columns(n):
                    return slice(n * SEG, (n + 1) * SEG)

                def norm_of(n):
                    return normalise(xT[:, :, columns(n)], xh[n % 2][:, :, :], (6, 7), True, x_ready[n],
                                     xh_free[n % 2], rstd[:, :])

                def down(n):
                    for k in range(KT):
                        bank = 4 + k
                        m = pe.do([mm(psum[bank][:, :], wd[:, j, k * P:(k + 1) * P], hid[n % 2][:, j, :], j == 0,
                                      j == FF // P - 1) for j in range(FF // P)], hdone[n], bank_free[bank])
                        bank_free[bank] = dve.do(tt(xT[:, k, columns(n)], xT[:, k, columns(n)], psum[bank][:, :],
                                                    ADD), m)
                    hid_free[n % 2] = m
                    added.append(bank_free[4 + KT - 1])

                for _ in norm_of(0):
                    pass
                h_ready = normalise.done
                for n in range(tiles):
                    s = n % 2
                    hdone[n] = []
                    ahead = norm_of(n + 1) if n + 1 < tiles else iter(())
                    for j in range(FF // P):
                        bg, bu = j % 2, 2 + j % 2
                        mg = pe.do([mm(psum[bg][:, :], wg[:, k, j * P:(j + 1) * P], xh[s][:, k, :], k == 0,
                                       k == KT - 1) for k in range(KT)], w, h_ready, bank_free[bg])
                        mu = pe.do([mm(psum[bu][:, :], wu[:, k, j * P:(j + 1) * P], xh[s][:, k, :], k == 0,
                                       k == KT - 1) for k in range(KT)], bank_free[bu])
                        m = act.do(fn(sg[j % 2][:, :], psum[bg][:, :], ACT.Silu), mg, sg_free[j % 2])
                        bank_free[bg] = m
                        m = dve.do(tt(hid[s][:, j, :], sg[j % 2][:, :], psum[bu][:, :], MUL), m, mu, hid_free[s])
                        bank_free[bu] = sg_free[j % 2] = m
                        hdone[n].append(m)
                        if j == 1 and n > 0:
                            down(n - 1)
                        if j > 1:
                            next(ahead, None)
                    for _ in ahead:
                        pass
                    xh_free[s] = mu
                    h_ready = normalise.done
                down(tiles - 1)
                return added

        fence()
        x_ready = swiglu("0", x_added)
        fence()

        with ExitStack() as mb:
            def sm(name, shape, dt=F32):
                return sb(name, shape, dt, mb)

            w_in = sm("w_in", [P, KT, 2 * DI])
            w_x = sm("w_x", [P, DT, NX])
            w_o = sm("w_o", [P, DT, HID])
            m_norm = sm("m_norm", [P, KT])
            m_taps = sm("m_taps", [P, DT, KC])
            m_cb = sm("m_cb", [P, DT])
            m_dtw = sm("m_dtw", [P, DT])
            m_dtb = sm("m_dtb", [P, DT])
            m_D = sm("m_D", [P, DT])
            m_A = sm("m_A", [P, DT, NS])
            u = sm("u", [P, KT, T])
            rstd = sm("rstd", [P, SEG])
            un = [sm(f"un{i}", [P, KT, SEG]) for i in range(2)]
            mraw = sm("mraw", [P, DT, HALO + T])
            xc = sm("xc", [P, DT, T])
            zs = sm("zs", [P, DT, T])
            xs = sm("xs", [NX, T])
            dtv = sm("dtv", [P, DT, T])
            dtu = sm("dtu", [P, DT, T])
            Bn = [sm(f"Bn{i}", [P, T]) for i in range(2)]
            Cn = [sm(f"Cn{i}", [P, T]) for i in range(2)]
            dA = [sm(f"dA{i}", [P, T]) for i in range(2)]
            dBu = [sm(f"dBu{i}", [P, T]) for i in range(2)]
            hs = [sm(f"hs{i}", [P, T]) for i in range(2)]
            hc = [sm(f"hc{i}", [P, T]) for i in range(2)]

            wl = load(sp, "mamba", [(w_in[:, :, :], a["w_in"]), (w_x[:, :, :], a["w_x"]), (w_o[:, :, :], a["w_o"]),
                                    (m_norm[:, :], a["m_norm"]), (m_taps[:, :, :], a["m_taps"]),
                                    (m_cb[:, :], a["m_cb"]), (m_dtw[:, :], a["m_dtw"]), (m_dtb[:, :], a["m_dtb"]),
                                    (m_D[:, :], a["m_D"]), (m_A[:, :, :], a["m_A"])])
            e1 = act.do(fn(m_A[:, :, :], m_A[:, :, :], ACT.Exp), wl)
            m_a_ready = dve.do(lambda e: e.tensor_scalar(m_A[:, :, :], m_A[:, :, :], -1.0, None, MUL), e1)
            halo = pool.do(lambda e: e.memset(mraw[:, :, 0:HALO], 0.0))
            m_ready = [None] * (NB * NSEG)
            u_free = un_free = raw_free2 = xc_free = zs_free = None
            scan_free = None
            bn_free, cn_free = [None, None], [None, None]
            da_free, dbu_free, hs_free, hc_free = [None] * 2, [None] * 2, [None] * 2, [None] * 2
            xs_free = None
            for b in range(NB):
                u_done, evac, zdone = [], [], []
                for n in range(NSEG):
                    cols = slice(n * SEG, (n + 1) * SEG)
                    xcols = slice(b * T + n * SEG, b * T + (n + 1) * SEG)
                    for _ in normalise(xT[:, :, xcols], u[:, :, cols], (6, 7), True, x_ready[b * NSEG + n], u_free,
                                       rstd[:, :]):
                        pass
                    u_done.append(normalise.done)
                    for _ in normalise(u[:, :, cols], un[n][:, :, :], (6, 7), False, normalise.done, un_free,
                                       rstd[:, :], m_norm[:, :]):
                        pass
                    un_done = normalise.done
                    for j in range(2 * DT):
                        bank = j % 4
                        m = pe.do([mm(psum[bank][:, :], w_in[:, k, j * P:(j + 1) * P], un[n][:, k, :], k == 0,
                                      k == KT - 1) for k in range(KT)], wl, un_done, bank_free[bank])
                        if j < DT:
                            bank_free[bank] = act.do(fn(mraw[:, j, HALO + n * SEG:HALO + (n + 1) * SEG],
                                                        psum[bank][:, :], ACT.Copy), m, raw_free2)
                            evac.append(bank_free[bank])
                        else:
                            bank_free[bank] = act.do(fn(zs[:, j - DT, cols], psum[bank][:, :], ACT.Silu), m, zs_free)
                            zdone.append(bank_free[bank])
                    un_last = m
                un_free = un_last
                xdone = []
                for j in range(DT):
                    m = dve.do(lambda e, j=j: e.tensor_scalar(xc[:, j, :], mraw[:, j, 0:T], m_taps[:, j, 0:1],
                                                              None, MUL), evac, halo, wl, xc_free)
                    for i in range(1, KC):
                        m = dve.do(lambda e, j=j, i=i: e.scalar_tensor_tensor(
                            xc[:, j, :], mraw[:, j, i:i + T], m_taps[:, j, i:i + 1], xc[:, j, :], MUL, ADD), m)
                    raw_free2 = m
                    xdone.append(act.do(fn(xc[:, j, :], xc[:, j, :], ACT.Silu, bias=m_cb[:, j:j + 1]), m))
                ssm = []
                for n in range(NSEG):
                    cols = slice(n * SEG, (n + 1) * SEG)
                    m = pe.do([mm(psum[n][0:NX, :], w_x[:, j, :], xc[:, j, cols], j == 0, j == DT - 1)
                               for j in range(DT)], xdone, bank_free[n])
                    bank_free[n] = act.do(fn(xs[:, cols], psum[n][0:NX, :], ACT.Copy), m, xs_free)
                    ssm.append(bank_free[n])
                stored = load(sp, f"scratch{b}", [(a["scratch"][b], xs[:, :])], ssm)
                xs_free = stored

                def rows(name, tile, r, *after):
                    return load(sp, name, [(tile[:, :], a["scratch"][b, r:r + 1, :].broadcast_to([P, T]))], *after)

                dt_in = rows("dt", dA[0], 2 * NS, stored, da_free[0])
                for j in range(DT):
                    m = act.do(fn(dA[1][:, :], dA[0][:, :], ACT.Abs, scale=m_dtw[:, j:j + 1], bias=m_dtb[:, j:j + 1]),
                               dt_in, wl, da_free[1])
                    r1 = dve.do(lambda e, j=j: e.tensor_scalar(dtv[:, j, :], dA[0][:, :], m_dtw[:, j:j + 1],
                                                               m_dtb[:, j:j + 1], MUL, ADD), dt_in, wl, scan_free)
                    r2 = dve.do(lambda e, j=j: e.tensor_scalar(dtv[:, j, :], dtv[:, j, :], 0.0, None, ALU.max), r1)
                    m = act.do(fn(dA[1][:, :], dA[1][:, :], ACT.Exp, scale=-1.0), m)
                    m = act.do(fn(dA[1][:, :], dA[1][:, :], ACT.Ln, bias=ONE), m)
                    m = dve.do(tt(dtv[:, j, :], dtv[:, j, :], dA[1][:, :], ADD), m, r2)
                    da_free[1] = m
                    dt_done = m
                    dtu_done = dve.do(tt(dtu[:, j, :], dtv[:, j, :], xc[:, j, :], MUL), m, xdone, scan_free)
                da_free[0] = r1
                count = 0
                started = [False] * 8
                for n in range(NS):
                    bs = rows(f"B{n % 2}", Bn[n % 2], n, stored, bn_free[n % 2])
                    cs = rows(f"C{n % 2}", Cn[n % 2], NS + n, cn_free[n % 2])
                    for j in range(DT):
                        k = count % 2
                        count += 1
                        m1 = act.do(fn(dA[k][:, :], dtv[:, j, :], ACT.Exp, scale=m_A[:, j, n:n + 1]), dt_done,
                                    m_a_ready, da_free[k])
                        m2 = pool.do(tt(dBu[k][:, :], dtu[:, j, :], Bn[n % 2][:, :], MUL), dtu_done, bs, dbu_free[k])
                        m3 = dve.do(lambda e, k=k: e.tensor_tensor_scan(hs[k][:, :], dA[k][:, :], dBu[k][:, :], 0.0,
                                                                        MUL, ADD), m1, m2, hs_free[k])
                        da_free[k] = dbu_free[k] = m3
                        m4 = dve.do(tt(hc[k][:, :], hs[k][:, :], Cn[n % 2][:, :], MUL), m3, cs, hc_free[k])
                        hs_free[k] = m4
                        m5 = pe.do([mm(psum[2 * j + q][:, :], eye[:, :], hc[k][:, q * SEG:(q + 1) * SEG], n == 0,
                                       n == NS - 1, loose=True) for q in range(NSEG)], m4,
                                   [bank_free[2 * j], bank_free[2 * j + 1]] if n == 0 else None)
                        hc_free[k] = m5
                    bn_free[n % 2], cn_free[n % 2] = m2, m4
                scan_free = m3
                for j in range(DT):
                    m = dve.do([lambda e, j=j, q=q: e.scalar_tensor_tensor(
                        xc[:, j, q * SEG:(q + 1) * SEG], xc[:, j, q * SEG:(q + 1) * SEG], m_D[:, j:j + 1],
                        psum[2 * j + q][:, :], MUL, ADD) for q in range(NSEG)], m5)
                    bank_free[2 * j] = bank_free[2 * j + 1] = m
                    m = dve.do(tt(xc[:, j, :], xc[:, j, :], zs[:, j, :], MUL), m, zdone)
                zs_free = m
                for n in range(NSEG):
                    cols = slice(n * SEG, (n + 1) * SEG)
                    xcols = slice(b * T + n * SEG, b * T + (n + 1) * SEG)
                    for k in range(KT):
                        bank = n * KT + k
                        mo = pe.do([mm(psum[bank][:, :], w_o[:, j, k * P:(k + 1) * P], xc[:, j, cols], j == 0,
                                       j == DT - 1) for j in range(DT)], m, bank_free[bank])
                        bank_free[bank] = dve.do(tt(xT[:, k, xcols], xT[:, k, xcols], psum[bank][:, :], ADD), mo)
                        m_ready[b * NSEG + n] = dve.do(tt(xT[:, k, xcols], xT[:, k, xcols], u[:, k, cols], ADD),
                                                       bank_free[bank], u_done)
                    u_free = m_ready[b * NSEG + n]
                xc_free = mo

        fence()
        final = swiglu("1", m_ready)
        outs = None
        for n in range(NB * T // SEG):
            cols = slice(n * SEG, (n + 1) * SEG)
            outs = load(sp, "out", [(out[:, :, cols], xT[:, :, cols])], final[n])
        sp.wait(outs)

        block = ctx.enter_context(nc.Block())

        @block.tensor
        def _(eng):
            pe.play(eng)

        @block.vector
        def _(eng):
            dve.play(eng)

        @block.scalar
        def _(eng):
            act.play(eng)

        @block.gpsimd
        def _(eng):
            pool.play(eng)

        @block.sync
        def _(eng):
            sp.play(eng)


def kernel(**inputs):
    import numpy as np
    import concourse.bacc as bacc
    from concourse.bass_utils import run_bass_kernel_spmd

    i = {k: np.asarray(v) for k, v in inputs.items()}
    A, B, FN = "L0_attn_a_", "L0_attn_b_", "L0_ffn_"

    def rows(w):
        return w.reshape(-1, P, w.shape[1]).transpose(1, 0, 2)

    x = i[A + "hidden_states"]
    heads = np.concatenate(
        [rows(i[A + w]).reshape(P, KT, H, P).transpose(2, 0, 1, 3).reshape(H, P, KT * P) for w in ("Wq", "Wk", "Wv")] +
        [i[A + "Wfb"].reshape(P, H, P).transpose(1, 0, 2)], axis=2)
    out_w = np.concatenate([i[A + "Wgb"].reshape(P, H, P).transpose(1, 0, 2), i[A + "Wo"].reshape(H, P, HID)], axis=2)
    conv = np.stack([i[A + c].reshape(H, P, KC) for c in ("conv_q", "conv_k", "conv_v")], axis=1)
    j, col = np.arange(P)[:, None] % SUBB, np.arange(SUBB)[None, :]
    masks = [j == col] + [(j // (2 * h) == col // (2 * h)) & (j // h % 2 == 0) & (col // h % 2 == 1) for h in LEVELS]
    arrays = {
        "xT": rows(x.reshape(NB * T, HID).T),
        "eye": np.eye(P, dtype=np.float32),
        "masks": np.stack(masks, axis=1).astype(np.float32),
        "head_w": heads,
        "out_w": out_w,
        "wfa": rows(i[A + "Wfa"]), "wga": rows(i[A + "Wga"]), "wb": rows(i[A + "Wb"]),
        "taps": conv.transpose(2, 0, 1, 3),
        "dt_bias": i[A + "dt_bias"].reshape(H, P).T,
        "a_log": np.broadcast_to(i[A + "A_log"].reshape(1, H), (P, H)),
        "norm_w": i[A + "norm_w"].reshape(P, 1),
        "w_gate": rows(i[FN + "w_gate"].T), "w_up": rows(i[FN + "w_up"].T), "w_down": rows(i[FN + "w_down"].T),
        "w_in": rows(i[B + "in_proj_w"].T), "w_x": rows(i[B + "x_proj_w"].T), "w_o": rows(i[B + "out_proj_w"].T),
        "m_norm": i[B + "norm_w"].reshape(KT, P).T,
        "m_taps": i[B + "conv_w"].reshape(DT, P, KC).transpose(1, 0, 2),
        "m_cb": i[B + "conv_b"].reshape(DT, P).T,
        "m_dtw": i[B + "dt_w"].reshape(DT, P).T,
        "m_dtb": i[B + "dt_b"].reshape(DT, P).T,
        "m_D": i[B + "D_param"].reshape(DT, P).T,
        "m_A": i[B + "A_log"].reshape(DT, P, NS).transpose(1, 0, 2),
    }
    arrays = {k: np.ascontiguousarray(v) for k, v in arrays.items()}
    nc = bacc.Bacc("TRN2", target_bir_lowering=False, num_devices=1)
    aps = {k: nc.dram_tensor("in_" + k, v.shape, mybir.dt.from_np(v.dtype), kind="ExternalInput").ap()
           for k, v in arrays.items()}
    aps["scratch"] = nc.dram_tensor("ssm_rows", (NB, NX, T), F32, kind="Internal").ap()
    out = nc.dram_tensor("out_xT", (P, KT, NB * T), F32, kind="ExternalOutput").ap()
    hybrid_block(nc, aps, out)
    r = run_bass_kernel_spmd(nc, [{"in_" + k: v for k, v in arrays.items()}], core_ids=[0])
    got = r.results[0]["out_xT"]
    return got.transpose(1, 0, 2).reshape(HID, NB, T).transpose(1, 2, 0)
```

```python
from contextlib import ExitStack

import concourse.bass as bass
from concourse import mybir

F32 = mybir.dt.float32
I32 = mybir.dt.int32
ALU = mybir.AluOpType
ACT = mybir.ActivationFunctionType
MUL, ADD, SUB = ALU.mult, ALU.add, ALU.subtract

P = 128
NB = 2
T = 1024
HID = 256
KT = HID // P
H = 16
KC = 4
HALO = KC - 1
CH = 64
SUBB = CH // 2
SEG = 512
NSEG = T // SEG
NC = SEG // CH
FF = 1024
DI = 512
DT = DI // P
NS = 16
NX = 2 * NS + 1
LEVELS = [1, 2, 4, 8, 16]
BANK = 512


class Lane:

    def __init__(self, sem, one_by_one=False):
        self.sem, self.count, self.program, self.waited = sem, 0, [], {}
        self.one_by_one = one_by_one

    def wait(self, *marks):
        need = {}
        for mark in marks:
            if isinstance(mark, list):
                for m in mark:
                    if m is not None:
                        need[m[0]] = max(need.get(m[0], 0), m[1])
            elif mark is not None:
                need[mark[0]] = max(need.get(mark[0], 0), mark[1])
        for sem, value in need.items():
            if self.waited.get(sem, 0) < value:
                self.waited[sem] = value
                self.program.append(lambda eng, sem=sem, value=value: eng.wait_ge(sem, value))

    def do(self, steps, *after):
        self.wait(*after)
        if not isinstance(steps, list):
            steps = [steps]
        if self.one_by_one:
            for step in steps[:-1]:
                self.wait((self.sem, self.count))
                self.count += 1
                self.program.append(lambda eng, step=step: step(eng).then_inc(self.sem, 1))
            self.wait((self.sem, self.count))
        else:
            self.program += steps[:-1]
        self.count += 1
        self.program.append(lambda eng, last=steps[-1]: last(eng).then_inc(self.sem, 1))
        return (self.sem, self.count)

    def play(self, eng):
        for step in self.program:
            step(eng)


def spread(ap, axis, n):
    a = ap.unsqueeze(axis)
    shape = list(a.shape)
    shape[axis] = n
    return a.broadcast_to(shape)


def braid(streams, lengths):
    live = [[name, gen, 0] for name, gen in streams]
    while live:
        item = min(live, key=lambda it: it[2] / lengths.get(it[0], 50))
        try:
            next(item[1])
            item[2] += 1
        except StopIteration:
            lengths[item[0]] = max(item[2], 1)
            live.remove(item)


def hybrid_block(nc, a, out):
    ctx = ExitStack()
    with ctx:
        def sb(name, shape, dt=F32, scope=ctx):
            return scope.enter_context(nc.sbuf_tensor(name, shape, dt))

        def sem(name):
            return ctx.enter_context(nc.semaphore(name))

        pe, dve, act, pool, sp = (Lane(sem("done_" + n), n == "gpsimd")
                                  for n in ("tensor", "vector", "scalar", "gpsimd", "sync"))
        psum = [ctx.enter_context(nc.psum_tensor(f"bank{i}", [P, BANK], F32)) for i in range(8)]
        bank_free = [None] * 8

        dma_total = {}

        def load(queue, name, pairs, *after):
            if name not in dma_total:
                dma_total[name] = [sem("dma_" + name), 0]
            entry = dma_total[name]
            queue.wait(*after)
            for dst, src in pairs:
                entry[1] += 16
                queue.program.append(lambda eng, d=dst, s=src, q=entry[0]: eng.dma_start(d, s).then_inc(q, 16))
            return (entry[0], entry[1])

        xT = sb("xT", [P, KT, NB * T])
        mean_w = sb("mean_w", [P, P])
        ones = sb("ones", [P, P])
        eye = sb("eye", [P, P])
        biases = sb("biases", [P, 4])
        cen = sb("cen", [P, KT, SEG])
        sq = sb("sq", [P, KT, SEG])

        loaded_x = load(sp, "x", [(xT[:, :, :], a["xT"])])
        loaded_eye = load(sp, "eye", [(eye[:, :], a["eye"])])
        const_ready = pool.do([lambda e: e.memset(mean_w[:, :], 1.0 / HID),
                               lambda e: e.memset(ones[:, :], 1.0),
                               lambda e: e.memset(biases[:, 0:1], 1e-5),
                               lambda e: e.memset(biases[:, 1:2], 1e-6),
                               lambda e: e.memset(biases[:, 2:3], 1.0),
                               lambda e: e.memset(biases[:, 3:4], P * 1e-6)])
        EPS5, EPS6, ONE, EPSQ = (biases[:, i:i + 1] for i in range(4))

        def mm(bank_ap, lhsT, rhs, start=True, stop=True, loose=False):
            return lambda e: e.matmul(bank_ap, lhsT, rhs, start=start, stop=stop, skip_group_check=loose)

        def tt(o, x, y, op):
            return lambda e: e.tensor_tensor(o, x, y, op)

        def fn(o, i, f, **kw):
            return lambda e: e.activation(o, i, f, **kw)

        def table_set(name):
            act.program.append(lambda e: e.preload_act_table_set(name))

        LN_EXP, SILU_TANH = "natural_log_exp_and_others", "silu_and_others"
        norm_free = [None, None]

        def normalise(src, dst, banks, center, ready, dst_free, rstd, weight=None):
            b0, b1 = banks
            if center:
                summed = pe.do([mm(psum[b0][:, :], mean_w[:, :], src[:, k, :], k == 0, k == KT - 1)
                                for k in range(KT)], ready, const_ready, bank_free[b0])
                yield
                centred = dve.do(tt(cen[:, :, :], src, spread(psum[b0][:, :], 1, KT), SUB), summed, norm_free[0])
                bank_free[b0] = centred
                base = cen[:, :, :]
            else:
                centred, base = ready, src
            yield
            squared = act.do(fn(sq[:, :, :], base, ACT.Square), centred, norm_free[1])
            yield
            varied = pe.do([mm(psum[b1][:, :], mean_w[:, :], sq[:, k, :], k == 0, k == KT - 1)
                            for k in range(KT)], squared, const_ready, bank_free[b1])
            norm_free[1] = varied
            yield
            logged = act.do(fn(rstd, psum[b1][:, :], ACT.Ln, bias=EPS5), varied, norm_free[0])
            bank_free[b1] = logged
            inv = act.do(fn(rstd, rstd, ACT.Exp, scale=-0.5), logged)
            yield
            if weight is None:
                done = dve.do(tt(dst, base, spread(rstd, 1, KT), MUL), inv, dst_free)
            else:
                done = dve.do([lambda e, k=k: e.scalar_tensor_tensor(
                    dst[:, k, :], base[:, k, :], weight[:, k:k + 1], rstd, MUL, MUL)
                    for k in range(KT)], inv, dst_free)
            norm_free[0] = done
            normalise.done = done
            yield

        with ExitStack() as att:
            def sa(name, shape, dt=F32):
                return sb(name, shape, dt, att)

            xn = sa("xn", [P, KT, NB, T])
            hfa = sa("hfa", [P, 2, SEG])
            hga = sa("hga", [P, 2, SEG])
            wfa = sa("wfa", [P, KT, P])
            wga = sa("wga", [P, KT, P])
            wb = sa("wb", [P, KT, H])
            masks = sa("masks", [P, 6, SUBB])
            taps = sa("taps", [P, H, 3, KC])
            dt_bias = sa("dt_bias", [P, H])
            neg_a = sa("neg_a", [P, H])
            norm_w = sa("norm_w", [P, 1])
            beta = sa("beta", [P, T // CH, H])
            tails = sa("tails", [P, H, 3, NB, HALO])
            W = [sa(f"W{i}", [P, 7 * P]) for i in range(2)]
            WO = [sa(f"WO{i}", [P, P + HID]) for i in range(2)]
            raw = [sa(f"raw{i}", [P, NB, HALO + SEG]) for i in range(2)]
            vc = sa("vc", [P, NC, NB, CH])
            tmp, tmp2 = cen, sq
            qn = [sa(f"qn{i}", [P, NC, NB, CH]) for i in range(2)]
            kL = [sa(f"kL{i}", [P, NC, NB, CH]) for i in range(2)]
            gate = [sa(f"gate{i}", [P, NC, NB, CH]) for i in range(2)]
            R = [sa(f"R{i}", [P, 2, NC, NB, CH]) for i in range(2)]
            vT = [sa(f"vT{i}", [P, NC, P]) for i in range(3)]
            kRT = sa("kRT", [P, NC, P])
            WT = [sa(f"WT{i}", [P, NC, P]) for i in range(2)]
            kT = [sa(f"kT{i}", [P, NC, P]) for i in range(2)]
            tot = {2 * h: sa(f"tot{2 * h}", [P, NB * SEG // (2 * h)]) for h in LEVELS}
            tot_chunk = [sa(f"tot_chunk{i}", [P, NC, NB]) for i in range(2)]
            Bd = sa("Bd", [P, NC, P])
            Xd = sa("Xd", [P, NC, P])
            Bt = sa("Bt", [P, NC, P])
            Xfull = sa("Xfull", [P, NC, P])
            Bc = sa("Bc", [P, NC, SUBB])
            Xc = sa("Xc", [P, NC, SUBB])
            X = sa("X", [P, NC, SUBB])
            bs = [sa(f"bs{i}", [P, NC]) for i in range(2)]
            knorm = sa("knorm", [P, 2, NC])
            Oc = sa("Oc", [P, NC, SUBB])
            bm = sa("bm", [P, NC, SUBB])
            Ac = sa("Ac", [P, NC, SUBB])
            AT = [sa(f"AT{i}", [P, NC, CH]) for i in range(2)]
            S = sa("S", [P, H, NB, P])
            Sx = sa("Sx", [P, NB, P])
            dpad = [sa(f"dpad{i}", [P, NB, P]) for i in range(2)]
            oT = sa("oT", [P, NC, NB, CH])

            PROJ = (0, 1, 5)
            PROD, INV, CHAIN = 2, 3, 4
            OUT = (6, 7)
            turn = [0]

            def flat(t):
                return t[:, :, :, :].rearrange("p c b t -> p (c b t)")

            def halves(t):
                return flat(t).rearrange("p (a n) -> p a n", a=2)

            def pair_cols(t, c):
                return t[:, c, :, :].rearrange("p b t -> p (b t)")

            def half_cols(t, seg, a):
                base = seg * SEG + a * 4 * CH
                return t[:, :, base:base + 4 * CH].rearrange("p b (c t) -> p c b t", t=CH)

            def proj_bank():
                turn[0] += 1
                return PROJ[turn[0] % len(PROJ)]

            small = load(sp, "small", [(wfa[:, :, :], a["wfa"]), (wga[:, :, :], a["wga"]), (wb[:, :, :], a["wb"]),
                                       (masks[:, :, :], a["masks"]), (taps[:, :, :, :], a["taps"]),
                                       (dt_bias[:, :], a["dt_bias"]), (neg_a[:, :], a["a_log"]),
                                       (norm_w[:, :], a["norm_w"])])
            w_loaded, wo_loaded, w_free, wo_free = {}, {}, [None, None], [None, None]

            def load_head(g):
                h = g % H
                w_loaded[g] = load(sp, f"w{g % 2}", [(W[g % 2][:, :], a["head_w"][h])], w_free[g % 2])

            load_head(0)

            zeroed = pool.do([lambda e, t=t: e.memset(t[:, :, :], 0.0)
                              for t in [Bd, Xd, Bt, Xfull, AT[0], AT[1], dpad[0], dpad[1]]])
            bank_zeroed = dve.do(lambda e: e.memset(psum[PROD][:, :], 0.0))
            bank_free[PROD] = bank_zeroed
            s_zeroed = dve.do(lambda e: e.memset(S[:, :, :, :], 0.0))
            expa = act.do(fn(neg_a[:, :], neg_a[:, :], ACT.Exp), small)
            table_set(LN_EXP)
            a_ready = dve.do(lambda e: e.tensor_scalar(neg_a[:, :], neg_a[:, :], -1.0, None, MUL), expa)

            nw_ready = dve.do(lambda e: e.tensor_scalar(norm_w[:, :], norm_w[:, :], 0.5, None, MUL), small)
            xn_ready = []
            xflat = xn[:, :, :, :].rearrange("p k b t -> p k (b t)")
            for n in range(NB * T // SEG):
                cols = slice(n * SEG, (n + 1) * SEG)
                for _ in normalise(xT[:, :, cols], xflat[:, :, cols],
                                   (2 * (n % 2), 2 * (n % 2) + 1), True, loaded_x, None,
                                   vc[:, 0:NC // NB, :, :].rearrange("p c b t -> p (c b t)")):
                    pass
                xn_ready.append(normalise.done)
            logits = pe.do([mm(psum[0][b * CH:(b + 1) * CH, c * H:(c + 1) * H], xn[:, k, b, c * CH:(c + 1) * CH],
                               wb[:, k, :], k == 0, k == KT - 1)
                            for c in range(T // CH) for b in range(NB) for k in range(KT)],
                           xn_ready, small, bank_free[0])
            beta_ready = act.do(fn(beta[:, :, :].rearrange("p c h -> p (c h)"), psum[0][:, 0:T // CH * H],
                                   ACT.Sigmoid), logits)
            bank_free[0] = beta_ready

            def low_rank(w, dst, seg, dst_free):
                marks = []
                for a2 in range(2):
                    bank = proj_bank()
                    m = pe.do([mm(psum[bank][:, :], w[:, k, :], half_cols(xn[:, k, :, :], seg, a2), k == 0,
                                  k == KT - 1) for k in range(KT)], xn_ready, small, bank_free[bank])
                    bank_free[bank] = act.do(fn(dst[:, a2, :], psum[bank][:, :], ACT.Copy), m, dst_free)
                    marks.append(bank_free[bank])
                return marks

            hfa_ready, hga_ready, hfa_read, hga_read = {}, {}, [None], [None]

            front_done, tree_done, state_done = {}, {}, {}
            raw_free = [None, None]
            last = {"knorm": None, "xc_read": None, "bc_read": None, "tree": None, "oT": None, "small": None}
            last["tmp"] = last["tmp2"] = last["vc"] = list(norm_free)

            def front(g):
                seg, h = divmod(g, H)
                s = g % 2
                if g + 1 < NSEG * H:
                    load_head(g + 1)
                w = W[s]
                if h == 0:
                    hfa_ready[seg] = low_rank(wfa, hfa, seg, hfa_read[0])
                cols = slice(seg * SEG, (seg + 1) * SEG)
                dsts = (qn[s], kL[s], vc)
                silued = [None] * 3
                slot_free = tree_done.get(g - 2, None)
                absd, relud = [], []

                def gate_product(b):
                    bank = proj_bank()
                    m = hfa_read[0] = pe.do(mm(psum[bank][:, :], w[:, 6 * P:7 * P], hfa[:, b, :]), w_loaded[g],
                                            hfa_ready[seg], bank_free[bank])
                    absd.append(act.do(fn(tmp2[:, b, :], psum[bank][:, :], ACT.Abs, bias=dt_bias[:, h:h + 1]), m,
                                       small, last["tmp2"]))
                    relud.append(dve.do(lambda e: e.tensor_scalar(
                        halves(gate[s])[:, b, :], psum[bank][:, :], dt_bias[:, h:h + 1], 0.0, ADD, ALU.max),
                        absd[-1], slot_free))
                    bank_free[bank] = relud[-1]

                halos, evacs = {}, {}

                def tap(kind, i):
                    return taps[:, h, kind, i:i + 1]

                def conv_out(kind):
                    return dsts[kind][:, :, :, :].rearrange("p c b t -> p b c t")

                def halo(kind):
                    rb = (3 * g + kind) % 2
                    if seg == 0:
                        halos[kind] = pool.do(lambda e: e.memset(raw[rb][:, :, 0:HALO], 0.0), raw_free[rb])
                    else:
                        halos[kind] = pool.do(lambda e: e.tensor_copy(raw[rb][:, :, 0:HALO], tails[:, h, kind, :, :]),
                                              raw_free[rb])
                    evacs[kind] = []

                def project(kind, b):
                    rb = (3 * g + kind) % 2
                    bank = proj_bank()
                    m = w_free[s] = pe.do([mm(psum[bank][:, :], w[:, (kind * KT + k) * P:(kind * KT + k + 1) * P],
                                              xn[:, k, b, cols], k == 0, k == KT - 1) for k in range(KT)],
                                          w_loaded[g], xn_ready, bank_free[bank])
                    copied = act.do(fn(raw[rb][:, b, HALO:], psum[bank][:, :], ACT.Copy), m, raw_free[rb])
                    bank_free[bank] = act.do(fn(conv_out(kind)[:, b, :, :],
                                                psum[bank][:, :].rearrange("p (c t) -> p c t", t=CH), ACT.Copy,
                                                scale=tap(kind, KC - 1)), small,
                                             last["vc"] if kind == 2 else slot_free)
                    evacs[kind] += [copied, bank_free[bank]]

                halo(0)
                for b in range(NB):
                    project(0, b)
                    yield
                for kind in range(3):
                    rb = (3 * g + kind) % 2
                    kept = None
                    if seg == 0:
                        kept = pool.do(lambda e, rb=rb, kind=kind: e.tensor_copy(
                            tails[:, h, kind, :, :], raw[rb][:, :, SEG:SEG + HALO]), evacs[kind])
                    if kind < 2:
                        halo(kind + 1)
                    m = evacs[kind]
                    for i in range(KC - 1):
                        if kind == 2 and i == 0:
                            squared = act.do(fn(tmp[:, :, :], halves(kL[s]), ACT.Square), silued[1], last["tmp"])
                        if kind == 2 and i == KC - 2:
                            bank = proj_bank()
                            tsq = tmp[:, :, :].rearrange("p a (c n) -> p (a c) n", n=P)
                            last["tmp"] = pe.do([mm(psum[bank][:, c:c + 1], tsq[:, c, :], ones[:, 0:1])
                                                 for c in range(NC)], squared, const_ready, bank_free[bank])
                            k_summed = bank_free[bank] = act.do(fn(knorm[:, 0, :], psum[bank][:, 0:NC], ACT.Copy),
                                                                last["tmp"], last["knorm"])
                        for b in range(NB):
                            m = dve.do(lambda e, rb=rb, kind=kind, i=i, b=b: e.scalar_tensor_tensor(
                                conv_out(kind)[:, b, :, :],
                                raw[rb][:, b, i:i + SEG].rearrange("p (c t) -> p c t", t=CH),
                                tap(kind, i), conv_out(kind)[:, b, :, :], MUL, ADD), m, halos[kind], small)
                            if b == 0:
                                yield
                        if i < NB:
                            if kind < 2:
                                project(kind + 1, i)
                            else:
                                gate_product(i)
                        yield
                    w_free[s] = hfa_read[0]
                    raw_free[rb] = [m, kept]
                    if kind == 0:
                        table_set(SILU_TANH)
                    silued[kind] = act.do(fn(dsts[kind][:, :, :, :], dsts[kind][:, :, :, :], ACT.Silu), m)
                    yield
                table_set(LN_EXP)
                m = act.do(fn(knorm[:, 0, :], knorm[:, 0, :], ACT.Ln, bias=EPS6), k_summed)
                inv2 = act.do(fn(bs[s][:, :], knorm[:, 0, :], ACT.Exp, scale=-1.0), m, slot_free)
                norm_k = act.do(fn(knorm[:, 1, :], knorm[:, 0, :], ACT.Exp, scale=0.5), m)
                bs_ready = dve.do(tt(bs[s][:, :], bs[s][:, :], beta[:, seg * NC:(seg + 1) * NC, h], MUL), inv2,
                                  beta_ready)
                m = act.do(fn(tmp2[:, :, :], tmp2[:, :, :], ACT.Exp, scale=-1.0), absd)
                m = act.do(fn(tmp2[:, :, :], tmp2[:, :, :], ACT.Ln, bias=ONE), m)
                yield
                m = dve.do(tt(halves(gate[s]), halves(gate[s]), tmp2[:, :, :], ADD), m, relud)
                last["tmp2"] = m
                gated = act.do(fn(flat(gate[s]), flat(gate[s]), ACT.Exp, scale=neg_a[:, h:h + 1]), m, a_ready)
                vt_free = state_done.get(g - 3, None)
                turned = []
                for half in range(2):
                    bank = proj_bank()
                    m = pe.do([lambda e, c=c, bank=bank: e.transpose(
                        psum[bank][:, (c % 4) * P:(c % 4 + 1) * P], pair_cols(vc, c), eye[:, :])
                        for c in range(4 * half, 4 * half + 4)], silued[2], loaded_eye, bank_free[bank])
                    last["vc"] = m
                    turned.append(dve.do(tt(vT[g % 3][:, 4 * half:4 * half + 4, :],
                                            psum[bank][:, :].rearrange("p (c d) -> p c d", c=4),
                                            spread(knorm[:, 1, 4 * half:4 * half + 4], 2, P), MUL),
                                         m, norm_k, vt_free))
                    bank_free[bank] = turned[-1]
                    yield
                last["knorm"] = turned[-1]
                t = halves(qn[s])
                squared = act.do(fn(tmp[:, :, :], t, ACT.Square), silued[0], last["tmp"])
                yield
                logs = []
                for b in range(NB):
                    bank = proj_bank()
                    m = pe.do(mm(psum[bank][:, :], ones[:, :], tmp[:, b, :]), squared, const_ready, bank_free[bank])
                    last["tmp"] = m
                    logs.append(act.do(fn(tmp2[:, b, :], psum[bank][:, :], ACT.Ln, bias=EPSQ, scale=float(P)), m,
                                       last["tmp2"]))
                    bank_free[bank] = logs[-1]
                    yield
                inv = act.do(fn(tmp2[:, :, :], tmp2[:, :, :], ACT.Exp, scale=-0.5), logs)
                m = pool.do(tt(t, t, tmp2[:, :, :], MUL), inv)
                last["tmp2"] = m
                normed = [m, silued[1], bs_ready]
                yield
                front_done[g] = normed + turned + [gated]
                yield

            def tree(g):
                seg, h = divmod(g, H)
                s = g % 2
                ready = front_done[g]
                r_free = state_done.get(g - 2, None)
                wo_loaded[g] = load(sp, f"wo{s}", [(WO[s][:, :], a["out_w"][h])], wo_free[s])
                Rf = R[s][:, :, :, :, :].rearrange("p a c b t -> p a (c b t)")
                Lf = flat(kL[s])
                beta_g = bs[s][:, :]
                bank = PROD

                def quad(w):
                    return slice(SUBB * w, SUBB * (w + 1))

                def block(t, c, b, u):
                    return t[:, c, b, u * SUBB:(u + 1) * SUBB]

                def block_r(c, b, u):
                    return R[s][:, :, c, b, u * SUBB:(u + 1) * SUBB]

                def product(half, r_ready, l_ready):
                    steps = []
                    for c in range(NC):
                        for w in range(4):
                            b, u = w // 2, w % 2
                            o, r = psum[bank][quad(w), c * CH:(c + 1) * CH], block_r(c, b, u)
                            if half > 1:
                                o = o.rearrange("p (a n two t) -> p a n two t", a=2, two=2, t=half)[:, :, :, 1, :]
                                r = r.rearrange("p a (n two t) -> p a n two t", two=2, t=half)[:, :, :, 1, :]
                            else:
                                o = o.rearrange("p (a i) -> p a i", a=2)
                            steps.append(mm(o, block(kL[s], c, b, u), r))
                    return pe.do(steps, r_ready, l_ready, bank_free[bank])

                view = psum[bank][:, :].rearrange("p (c a i) -> p c a i", c=NC, a=2)
                inv_x = psum[INV][:, 0:NC * SUBB].rearrange("p (c i) -> p c i", c=NC)

                def mask(li):
                    return spread(masks[:, li, :], 1, NC)

                def blocks(lhsT, rhs, *after):
                    return pe.do([mm(psum[INV][quad(w), c * SUBB:(c + 1) * SUBB], lhsT[:, c, quad(w)], rhs(c))
                                  for c in range(NC) for w in range(4)], *after)

                def on_diagonal(dst, src, *after):
                    return act.do([fn(dst[quad(w), :, quad(w)], src[quad(w), :, :], ACT.Copy) for w in range(4)],
                                  zeroed, *after)

                def x_transposed(dst, x_made, dst_free):
                    m = dve.do(lambda e: e.transpose(Xc[:, :, :].rearrange("p c i -> p (c i)"),
                                                     X[:, :, :].rearrange("p c i -> p (c i)")),
                               x_made, last["xc_read"])
                    last["xc_read"] = on_diagonal(dst, Xc, m, dst_free)
                    return last["xc_read"]

                prod = pe.do([mm(psum[bank][quad(2 * b + u), c * SUBB:(c + 1) * SUBB], block(kL[s], c, b, u),
                                 block(qn[s], c, b, u)) for c in range(NC) for b in range(NB) for u in range(2)],
                             ready, bank_free[bank])
                rk = dve.do(tt(Rf[:, 0, :], Lf, flat(gate[s]), MUL), ready, r_free)
                rq = pool.do(tt(Rf[:, 1, :], flat(qn[s]), flat(gate[s]), MUL), ready, r_free)
                acc = dve.do(tt(Ac[:, :, :], psum[bank][:, 0:NC * SUBB].rearrange("p (c i) -> p c i", c=NC),
                                mask(0), MUL), prod, small, last["tree"])
                bank_free[bank] = acc
                r_ready, l_ready = [rk, rq], ready
                t_ready, t_now = ready, flat(gate[s])
                tree_free = last["tree"]
                yield
                p1 = oc = xs = xd = bm_free = None
                x_free = bd_free = tree_free

                def x_product():
                    return blocks(Xd, lambda c: Oc[:, c, :], oc, xd)

                def x_update(p2):
                    xs = dve.do(tt(X[:, :, :], X[:, :, :], inv_x, SUB), p2)
                    bank_free[INV] = xs
                    return xs

                for li, half in enumerate(LEVELS):
                    prod = product(half, r_ready, l_ready)
                    bmd = pool.do(tt(bm[:, :, :], mask(1 + li), spread(beta_g, 2, SUBB), MUL),
                                  ready, small, bm_free, last["small"])
                    yield
                    pair = t_now.rearrange("p (n two) -> p n two", two=2)
                    Rv = Rf.rearrange("p a (n two t) -> p a n two t", two=2, t=half)
                    Lv = Lf.rearrange("p (n two t) -> p n two t", two=2, t=half)
                    up_t = (pool if half > 1 else dve).do(
                        tt(tot[2 * half][:, :], pair[:, :, 0], pair[:, :, 1], MUL), t_ready, tree_free)
                    up_q = pool.do(tt(Rv[:, 1, :, 1, :], Rv[:, 1, :, 1, :], spread(pair[:, :, 0], 2, half), MUL),
                                   prod, t_ready)
                    if half > 2:
                        p2 = x_free = x_product()
                    up_k = dve.do(tt(Rv[:, 0, :, 1, :], Rv[:, 0, :, 1, :], spread(pair[:, :, 0], 2, half), MUL),
                                  prod, t_ready)
                    up_l = (pool if half > 1 else dve).do(
                        tt(Lv[:, :, 0, :], Lv[:, :, 0, :], spread(pair[:, :, 1], 2, half), MUL), prod, t_ready)
                    r_ready, l_ready, t_ready, t_now = [up_q, up_k], up_l, up_t, tot[2 * half][:, :]
                    yield
                    if half > 2:
                        xs = x_update(p2)
                    bm_free = dve.do(tt(Bc[:, :, :], view[:, :, 0, :], bm[:, :, :], MUL), prod, bmd,
                                     last["bc_read"])
                    bd = last["bc_read"] = on_diagonal(Bd, Bc, bm_free, bd_free)
                    yield
                    acc = dve.do(lambda e, li=li: e.copy_predicated(
                        Ac[:, :, :], mask(1 + li).bitcast(I32), view[:, :, 1, :]), acc, prod)
                    bank_free[bank] = acc
                    last["small"] = bm_free
                    yield
                    rhs = (lambda c: masks[:, 0, :]) if half == 1 else (lambda c: X[:, c, :])
                    p1 = blocks(Bd, rhs, bd, xs, bank_free[INV])
                    bd_free = p1
                    if half > 1:
                        xd = x_transposed(Xd, xs, x_free)
                    if half == 1:
                        xs = dve.do(tt(X[:, :, :], mask(0), inv_x, SUB), p1, x_free)
                        bank_free[INV] = xs
                    else:
                        oc = act.do(fn(Oc[:, :, :], inv_x, ACT.Copy), p1, x_free)
                    yield
                prod = pe.do([mm(psum[bank][quad(2 * b), c * CH:(c + 1) * CH], block(kL[s], c, b, 0),
                                 block_r(c, b, 1)) for c in range(NC) for b in range(NB)],
                             r_ready, l_ready, bank_free[bank])
                p2 = x_product()
                xs = x_update(p2)
                pair = t_now.rearrange("p (n two) -> p n two", two=2)
                Rv = Rf.rearrange("p a (n two t) -> p a n two t", two=2, t=SUBB)
                Lv = Lf.rearrange("p (n two t) -> p n two t", two=2, t=SUBB)
                up_q = pool.do(tt(Rv[:, 1, :, 1, :], Rv[:, 1, :, 1, :], spread(pair[:, :, 0], 2, SUBB), MUL),
                               prod, t_ready)
                up_l = pool.do(tt(Lv[:, :, 0, :], Lv[:, :, 0, :], spread(pair[:, :, 1], 2, SUBB), MUL), prod, t_ready)
                up_t = pool.do(tt(tot_chunk[s][:, :, :].rearrange("p c b -> p (c b)"), pair[:, :, 0], pair[:, :, 1],
                                  MUL), t_ready, r_free)
                scaled = pool.do(tt(Ac[:, :, :], Ac[:, :, :], spread(beta_g, 2, SUBB), MUL), acc)
                bt = dve.do([tt(Bt[quad(w), :, quad(w + 1)], view[quad(w), :, 0, :],
                                spread(beta_g[quad(w), :], 2, SUBB), MUL) for w in (0, 2)], prod, zeroed, tree_free)
                yield
                p1 = blocks(Bt, lambda c: X[:, c, :], bt, xs, bank_free[INV])
                xd = x_transposed(Xfull, xs, tree_free)
                up_k = dve.do(tt(Rv[:, 0, :, 1, :], Rv[:, 0, :, 1, :], spread(pair[:, :, 0], 2, SUBB), MUL),
                              prod, t_ready)
                at = dve.do([tt(AT[s][quad(w), :, SUBB:CH], view[quad(w), :, 1, :],
                                spread(beta_g[quad(w), :], 2, SUBB), MUL) for w in (0, 2)], zeroed, r_free)
                bank_free[bank] = at
                oc = act.do(lambda e: e.activation(Oc[:, :, :], inv_x, ACT.Copy, scale=-1.0), p1, p2)
                yield
                p2 = blocks(Xfull, lambda c: Oc[:, c, :], oc, xd)
                low = act.do([lambda e, w=w: e.activation(
                    AT[s][quad(w), :, SUBB * (w % 2):SUBB * (w % 2 + 1)], Ac[quad(w), :, :], ACT.Copy)
                    for w in range(4)], scaled, zeroed, r_free)
                yield
                xc_ = dve.do(lambda e: e.tensor_copy(X[:, :, :], inv_x), p2)
                bank_free[INV] = xc_
                xf = dve.do([lambda e, w=w: e.transpose(Xfull[quad(w - 1), :, quad(w)], X[quad(w), :, :])
                             for w in (1, 3)], xc_)
                yield
                turned = []
                for q in range(2):
                    b2 = proj_bank()
                    m = pe.do([lambda e, c=c, b2=b2: e.transpose(
                        psum[b2][:, (c % 4) * P:(c % 4 + 1) * P],
                        R[s][:, 0, c, :, :].rearrange("p b t -> p (b t)"), eye[:, :])
                        for c in range(4 * q, 4 * q + 4)], up_k, loaded_eye, bank_free[b2])
                    turned.append(act.do(fn(kRT[:, 4 * q:4 * q + 4, :].rearrange("p c d -> p (c d)"),
                                            psum[b2][:, :], ACT.Copy), m, tree_free))
                    bank_free[b2] = turned[-1]
                yield
                keyed = []
                for q in range(2):
                    b2 = proj_bank()
                    m = pe.do([lambda e, c=c, b2=b2: e.transpose(
                        psum[b2][:, (c % 4) * P:(c % 4 + 1) * P], pair_cols(kL[s], c), eye[:, :])
                        for c in range(4 * q, 4 * q + 4)], up_l, bank_free[b2])
                    keyed.append(dve.do(tt(kT[s][:, 4 * q:4 * q + 4, :],
                                           psum[b2][:, :].rearrange("p (c d) -> p c d", c=4),
                                           spread(beta_g[:, 4 * q:4 * q + 4], 2, P), MUL), m, r_free))
                    bank_free[b2] = keyed[-1]
                yield
                solved = []
                for q in range(2):
                    b2 = proj_bank()
                    m = pe.do([mm(psum[b2][:, (c % 4) * P:(c % 4 + 1) * P], Xfull[:, c, :], vT[g % 3][:, c, :])
                               for c in range(4 * q, 4 * q + 4)], xf, xd, ready, bank_free[b2])
                    solved.append(act.do(fn(vT[g % 3][:, 4 * q:4 * q + 4, :].rearrange("p c d -> p (c d)"),
                                            psum[b2][:, :], ACT.Copy), m))
                    bank_free[b2] = solved[-1]
                    b2 = proj_bank()
                    m = pe.do([mm(psum[b2][:, (c % 4) * P:(c % 4 + 1) * P], kRT[:, c, :], Xfull[:, c, :])
                               for c in range(4 * q, 4 * q + 4)], turned, bank_free[b2])
                    solved.append(act.do(fn(WT[s][:, 4 * q:4 * q + 4, :].rearrange("p c d -> p (c d)"),
                                            psum[b2][:, :], ACT.Copy), m, r_free))
                    bank_free[b2] = solved[-1]
                    yield
                last["tree"] = [xf, at, low, xd, p2, up_t, m]
                tree_done[g] = [up_q, up_k, up_t, low, at, xf, m] + keyed + solved
                yield

            s_ready = {h: [s_zeroed, s_zeroed] for h in range(H)}
            dpad_free = [None, None]
            chain = {}
            x_added = [None] * (NB * NSEG)

            def state(g):
                seg, h = divmod(g, H)
                s = g % 2
                ready = tree_done[g]
                upd = s_ready[h]
                o_evac = []
                if h == 0:
                    hga_ready[seg] = low_rank(wga, hga, seg, hga_read[0])
                tanh_g = R[s][:, 0, :, :, :].rearrange("p c b t -> p (c b t)").rearrange("p (a n) -> p a n", a=2)
                for c in range(NC):
                    if c == 3:
                        table_set(SILU_TANH)
                        tanhed = []
                        for a2 in range(2):
                            bank = proj_bank()
                            hga_read[0] = pe.do(mm(psum[bank][:, :], WO[s][:, 0:P], hga[:, a2, :]), wo_loaded[g],
                                                hga_ready[seg], bank_free[bank])
                            tanhed.append(act.do(fn(tanh_g[:, a2, :], psum[bank][:, :], ACT.Tanh, scale=0.5),
                                                 hga_read[0], ready))
                            bank_free[bank] = tanhed[-1]
                    src = S[:, h, :, :] if c % 2 == 0 else Sx[:, :, :]
                    dst = Sx[:, :, :] if c % 2 == 0 else S[:, h, :, :]
                    d = dpad[c % 2]
                    ob = OUT[c // 4]
                    ocol = lambda b, c=c: slice((c % 4) * P + b * CH, (c % 4) * P + (b + 1) * CH)
                    pred = pe.do([mm(psum[CHAIN][b * CH:(b + 1) * CH, 0:P], WT[s][:, c, b * CH:(b + 1) * CH],
                                     src[:, b, :]) for b in range(NB)], ready, upd, bank_free[CHAIN])
                    seen = pe.do([mm(psum[ob][:, ocol(b)], src[:, b, :], R[s][:, 1, c, b, :],
                                     start=(c % 4 == 0 and b == 0), stop=False, loose=True) for b in range(NB)],
                                 bank_free[ob])
                    dd = dve.do([tt(d[b * CH:(b + 1) * CH, b, :], vT[g % 3][b * CH:(b + 1) * CH, c, :],
                                    psum[CHAIN][b * CH:(b + 1) * CH, 0:P], SUB) for b in range(NB)],
                                pred, ready, zeroed, dpad_free[c % 2])
                    bank_free[CHAIN] = dd
                    yield
                    outer = pe.do(mm(psum[CHAIN][:, P:(1 + NB) * P], kT[s][:, c, :],
                                     d[:, :, :].rearrange("p b v -> p (b v)")), dd)
                    within = pe.do([mm(psum[ob][:, ocol(b)], d[:, b, :], AT[s][:, c, :], start=False, stop=True,
                                       loose=True) for b in range(NB)])
                    upd = dve.do([lambda e, b=b, src=src, dst=dst, c=c: e.scalar_tensor_tensor(
                        dst[:, b, :], src[:, b, :], tot_chunk[s][:, c, b:b + 1],
                        psum[CHAIN][:, (1 + b) * P:(2 + b) * P], MUL, ADD) for b in range(NB)], outer, seen)
                    bank_free[CHAIN] = upd
                    dpad_free[c % 2] = within
                    if c % 4 == 3:
                        k = c // 4
                        m = act.do(fn(halves(oT)[:, k, :], psum[ob][:, :], ACT.Copy), within, last["oT"])
                        bank_free[ob] = m
                        o_evac.append(m)
                    yield
                s_ready[h] = upd
                tmp3 = WT[s][:, :, :].rearrange("p c d -> p (c d)").rearrange("p (a n) -> p a n", a=2)
                tmp4 = R[s][:, 1, :, :, :].rearrange("p c b t -> p (c b t)").rearrange("p (a n) -> p a n", a=2)
                oh = halves(oT)
                table_set(LN_EXP)
                squared = act.do(fn(tmp3, oh, ACT.Square), o_evac, within)
                yield
                logs = []
                for b in range(NB):
                    bank = proj_bank()
                    m = pe.do(mm(psum[bank][:, :], ones[:, :], tmp3[:, b, :]), squared, bank_free[bank])
                    logs.append(act.do(fn(tmp4[:, b, :], psum[bank][:, :], ACT.Ln, bias=EPS6, scale=1.0 / P), m,
                                       within))
                    bank_free[bank] = logs[-1]
                inv = act.do(fn(tmp4, tmp4, ACT.Exp, scale=-0.5), logs)
                yield
                m = dve.do(lambda e: e.scalar_tensor_tensor(tmp4, tanh_g, 1.0, tmp4, ADD, MUL), inv, tanhed)
                m = dve.do(lambda e: e.scalar_tensor_tensor(oh, oh, norm_w[:, 0:1], tmp4, MUL, MUL), m, nw_ready)
                scratch_read = gated = m
                yield
                for b in range(NB):
                    for k in range(KT):
                        bank = proj_bank()
                        m = pe.do(mm(psum[bank][:, :], WO[s][:, (k + 1) * P:(k + 2) * P], oh[:, b, :]), gated,
                                  bank_free[bank])
                        dst = half_cols(xT[:, k, :].rearrange("p (b t) -> p b t", b=NB), seg, b)
                        bank_free[bank] = dve.do(tt(dst, dst, psum[bank][:, :].rearrange(
                            "p (c b t) -> p c b t", b=NB, t=CH), ADD), m, chain.get((b, k)))
                        chain[(b, k)] = bank_free[bank]
                        x_added[seg] = x_added[NSEG + seg] = bank_free[bank]
                    yield
                last["oT"] = m
                wo_free[s] = m
                state_done[g] = [upd, within, scratch_read]

            lengths = {}
            NG = NSEG * H
            for step in range(NG + 2):
                streams = []
                if step >= 2:
                    streams.append(("state", state(step - 2)))
                if 1 <= step <= NG:
                    streams.append(("tree", tree(step - 1)))
                if step < NG:
                    streams.append(("front", front(step)))
                braid(streams, lengths)

        def fence():
            marks = [(lane.sem, lane.count) for lane in (pe, dve, act, pool) if lane.count]
            for lane in (pe, dve, act, pool, sp):
                lane.wait(marks)
            return marks

        def swiglu(tag, x_ready):
            with ExitStack() as ff:
                wg = sb("wg" + tag, [P, KT, FF], F32, ff)
                wu = sb("wu" + tag, [P, KT, FF], F32, ff)
                wd = sb("wd" + tag, [P, FF // P, HID], F32, ff)
                xh = [sb(f"xh{i}" + tag, [P, KT, SEG], F32, ff) for i in range(2)]
                hid = [sb(f"hid{i}" + tag, [P, FF // P, SEG], F32, ff) for i in range(2)]
                rstd = sb("rstd" + tag, [P, SEG], F32, ff)
                sg = [sb(f"sg{i}" + tag, [P, SEG], F32, ff) for i in range(2)]
                w = load(sp, "ffn" + tag, [(wg[:, :, :], a["w_gate"]), (wu[:, :, :], a["w_up"]),
                                           (wd[:, :, :], a["w_down"])])
                xh_free, hid_free, sg_free = [None] * 2, [None] * 2, [None] * 2
                added, hdone = [], {}
                tiles = NB * T // SEG

                def columns(n):
                    return slice(n * SEG, (n + 1) * SEG)

                def norm_of(n):
                    return normalise(xT[:, :, columns(n)], xh[n % 2][:, :, :], (6, 7), True, x_ready[n],
                                     xh_free[n % 2], rstd[:, :])

                def down(n):
                    for k in range(KT):
                        bank = 4 + k
                        m = pe.do([mm(psum[bank][:, :], wd[:, j, k * P:(k + 1) * P], hid[n % 2][:, j, :], j == 0,
                                      j == FF // P - 1) for j in range(FF // P)], hdone[n], bank_free[bank])
                        bank_free[bank] = dve.do(tt(xT[:, k, columns(n)], xT[:, k, columns(n)], psum[bank][:, :],
                                                    ADD), m)
                    hid_free[n % 2] = m
                    added.append(bank_free[4 + KT - 1])

                for _ in norm_of(0):
                    pass
                h_ready = normalise.done
                for n in range(tiles):
                    s = n % 2
                    hdone[n] = []
                    ahead = norm_of(n + 1) if n + 1 < tiles else iter(())
                    for j in range(FF // P):
                        bg, bu = j % 2, 2 + j % 2
                        mg = pe.do([mm(psum[bg][:, :], wg[:, k, j * P:(j + 1) * P], xh[s][:, k, :], k == 0,
                                       k == KT - 1) for k in range(KT)], w, h_ready, bank_free[bg])
                        mu = pe.do([mm(psum[bu][:, :], wu[:, k, j * P:(j + 1) * P], xh[s][:, k, :], k == 0,
                                       k == KT - 1) for k in range(KT)], bank_free[bu])
                        m = act.do(fn(sg[j % 2][:, :], psum[bg][:, :], ACT.Silu), mg, sg_free[j % 2])
                        bank_free[bg] = m
                        m = dve.do(tt(hid[s][:, j, :], sg[j % 2][:, :], psum[bu][:, :], MUL), m, mu, hid_free[s])
                        bank_free[bu] = sg_free[j % 2] = m
                        hdone[n].append(m)
                        if j == 1 and n > 0:
                            down(n - 1)
                        if j > 1:
                            next(ahead, None)
                    for _ in ahead:
                        pass
                    xh_free[s] = mu
                    h_ready = normalise.done
                down(tiles - 1)
                return added

        fence()
        x_ready = swiglu("0", x_added)
        fence()

        with ExitStack() as mb:
            def sm(name, shape, dt=F32):
                return sb(name, shape, dt, mb)

            w_in = sm("w_in", [P, KT, 2 * DI])
            w_x = sm("w_x", [P, DT, NX])
            w_o = sm("w_o", [P, DT, HID])
            m_norm = sm("m_norm", [P, KT])
            m_taps = sm("m_taps", [P, DT, KC])
            m_cb = sm("m_cb", [P, DT])
            m_dtw = sm("m_dtw", [P, DT])
            m_dtb = sm("m_dtb", [P, DT])
            m_D = sm("m_D", [P, DT])
            m_A = sm("m_A", [P, DT, NS])
            mu = [sm(f"mu{i}", [P, KT, SEG]) for i in range(3)]
            rstd = sm("rstd", [P, SEG])
            un = sm("un", [P, KT, SEG])
            mraw = [sm(f"mraw{i}", [P, HALO + SEG]) for i in range(2)]
            mtails = sm("mtails", [P, DT, HALO])
            xc = [sm(f"xc{i}", [P, DT, SEG]) for i in range(2)]
            zs = [sm(f"zs{i}", [P, DT, SEG]) for i in range(2)]
            xs = sm("xs", [NX, SEG])
            dt_row = sm("dt_row", [P, SEG])
            soft = [sm(f"soft{i}", [P, SEG]) for i in range(2)]
            dtv = [sm(f"dtv{i}", [P, DT, SEG]) for i in range(2)]
            dtu = [sm(f"dtu{i}", [P, DT, SEG]) for i in range(2)]
            y = sm("y", [P, DT, SEG])
            diag_d = sm("diag_d", [P, DT, P])
            carry = sm("carry", [P, NS * DT])
            DEEP = 4
            Bn = [sm(f"Bn{i}", [P, SEG]) for i in range(DEEP)]
            Cn = [sm(f"Cn{i}", [P, SEG]) for i in range(DEEP)]
            AHEAD, LEAD = DEEP + 2, DT
            dA = [sm(f"dA{i}", [P, SEG]) for i in range(AHEAD)]
            dBu = [sm(f"dBu{i}", [P, SEG]) for i in range(AHEAD)]
            hs = [sm(f"hs{i}", [P, SEG]) for i in range(DEEP)]
            hc = [sm(f"hc{i}", [P, SEG]) for i in range(AHEAD)]

            wl = load(sp, "mamba", [(w_in[:, :, :], a["w_in"]), (w_x[:, :, :], a["w_x"]), (w_o[:, :, :], a["w_o"]),
                                    (m_norm[:, :], a["m_norm"]), (m_taps[:, :, :], a["m_taps"]),
                                    (m_cb[:, :], a["m_cb"]), (m_dtw[:, :], a["m_dtw"]), (m_dtb[:, :], a["m_dtb"]),
                                    (m_D[:, :], a["m_D"]), (m_A[:, :, :], a["m_A"])])
            e1 = act.do(fn(m_A[:, :, :], m_A[:, :, :], ACT.Exp), wl)
            m_a_ready = dve.do(lambda e: e.tensor_scalar(m_A[:, :, :], m_A[:, :, :], -1.0, None, MUL), e1)
            d_ready = dve.do([lambda e, j=j: e.tensor_scalar(diag_d[:, j, :], eye[:, :], m_D[:, j:j + 1], None, MUL)
                              for j in range(DT)], wl, loaded_eye)
            UNITS = NB * NSEG
            Y_BANKS, F_BANKS, O_BANKS = (0, 1, 2, 3), (4, 5), (6, 7)
            f_turn = [0]
            front_ready, scan_done, gated_y, m_ready, mu_ready = {}, {}, {}, {}, {}
            mraw_free, soft_free = [None] * 2, [None] * 2
            free = {"un": None, "tails": None, "xs": None, "dt_row": None}
            bn_free, cn_free = [None] * DEEP, [None] * DEEP
            da_free, dbu_free = [None] * AHEAD, [None] * AHEAD
            hs_free, hc_free = [None] * DEEP, [None] * AHEAD

            def f_bank():
                f_turn[0] += 1
                return F_BANKS[f_turn[0] % 2]

            def apart(steps):
                for _ in steps:
                    yield
                    yield

            def mamba_front(unit):
                b, n = divmod(unit, NSEG)
                s = unit % 2
                xcols = slice(unit * SEG, (unit + 1) * SEG)
                slot_free = [*scan_done.get(unit - 2, []), gated_y.get(unit - 2)]
                u = mu[unit % 3]
                yield from apart(normalise(xT[:, :, xcols], u[:, :, :], F_BANKS, True, x_ready[unit],
                                           m_ready.get(unit - 3), rstd[:, :]))
                mu_ready[unit] = normalise.done
                yield from apart(normalise(u[:, :, :], un[:, :, :], F_BANKS, False, mu_ready[unit], free["un"],
                                           rstd[:, :], m_norm[:, :]))
                un_done = normalise.done
                convolved = []
                for j in range(DT):
                    raw_j, rb = mraw[j % 2], j % 2
                    if n == 0:
                        halo = pool.do(lambda e, raw_j=raw_j: e.memset(raw_j[:, 0:HALO], 0.0), mraw_free[rb])
                    else:
                        halo = pool.do(lambda e, raw_j=raw_j, j=j: e.tensor_copy(raw_j[:, 0:HALO], mtails[:, j, :]),
                                       mraw_free[rb])
                    bank = f_bank()
                    m = pe.do([mm(psum[bank][:, :], w_in[:, k, j * P:(j + 1) * P], un[:, k, :], k == 0, k == KT - 1)
                               for k in range(KT)], wl, un_done, bank_free[bank])
                    copied = act.do(fn(raw_j[:, HALO:], psum[bank][:, :], ACT.Copy), m, mraw_free[rb])
                    bank_free[bank] = act.do(fn(xc[s][:, j, :], psum[bank][:, :], ACT.Copy,
                                                scale=m_taps[:, j, KC - 1:KC]), slot_free)
                    kept = None
                    if n + 1 < NSEG:
                        kept = pool.do(lambda e, raw_j=raw_j, j=j: e.tensor_copy(mtails[:, j, :],
                                                                                raw_j[:, SEG:SEG + HALO]), copied)
                    yield
                    m = [copied, bank_free[bank], halo]
                    for i in range(KC - 1):
                        m = dve.do(lambda e, i=i, j=j, raw_j=raw_j: e.scalar_tensor_tensor(
                            xc[s][:, j, :], raw_j[:, i:i + SEG], m_taps[:, j, i:i + 1], xc[s][:, j, :], MUL, ADD), m)
                        yield
                    mraw_free[rb] = [m, kept]
                    convolved.append(m)
                assert unit < 2 or unit - 2 in m_ready
                gates = []
                for j in range(DT):
                    bank = (F_BANKS + O_BANKS)[j]
                    gates.append(pe.do([mm(psum[bank][:, :], w_in[:, k, (DT + j) * P:(DT + j + 1) * P], un[:, k, :],
                                           k == 0, k == KT - 1) for k in range(KT)], un_done, bank_free[bank]))
                    if j % 2 == 1:
                        yield
                free["un"] = gates[-1]
                yield
                table_set(SILU_TANH)
                for j in range(DT):
                    x_silued = act.do(fn(xc[s][:, j, :], xc[s][:, j, :], ACT.Silu, bias=m_cb[:, j:j + 1]),
                                      convolved[j])
                for j in range(DT):
                    bank = (F_BANKS + O_BANKS)[j]
                    bank_free[bank] = z_silued = act.do(fn(zs[s][:, j, :], psum[bank][:, :], ACT.Silu), gates[j],
                                                        slot_free)
                table_set(LN_EXP)
                yield
                bank = f_bank()
                m = pe.do([mm(psum[bank][0:NX, :], w_x[:, j, :], xc[s][:, j, :], j == 0, j == DT - 1)
                           for j in range(DT)], x_silued, bank_free[bank])
                bank_free[bank] = act.do(fn(xs[:, :], psum[bank][0:NX, :], ACT.Copy), m, free["xs"])
                stored = load(sp, f"scratch{unit}", [(a["scratch"][unit], xs[:, :])], bank_free[bank])
                free["xs"] = stored
                dt_in = load(sp, "dt", [(dt_row[:, :], a["scratch"][unit, 2 * NS:NX, :].broadcast_to([P, SEG]))],
                             stored, free["dt_row"])
                for _ in range(6):
                    yield
                for j in range(DT):
                    f = soft[j % 2]
                    m = act.do(fn(f[:, :], dt_row[:, :], ACT.Abs, scale=m_dtw[:, j:j + 1], bias=m_dtb[:, j:j + 1]),
                               dt_in, wl, soft_free[j % 2])
                    r = act.do(fn(dtv[s][:, j, :], dt_row[:, :], ACT.Relu, scale=m_dtw[:, j:j + 1],
                                  bias=m_dtb[:, j:j + 1]), slot_free)
                    m = act.do(fn(f[:, :], f[:, :], ACT.Exp, scale=-1.0), m)
                    m = act.do(fn(f[:, :], f[:, :], ACT.Ln, bias=ONE), m)
                    yield
                    dt_done = soft_free[j % 2] = dve.do(tt(dtv[s][:, j, :], dtv[s][:, j, :], f[:, :], ADD), m, r)
                    yield
                    dtu_done = pool.do(tt(dtu[s][:, j, :], dtv[s][:, j, :], xc[s][:, j, :], MUL), dt_done, x_silued,
                                       slot_free)
                    yield
                free["dt_row"] = r
                front_ready[unit] = {"stored": stored, "dt": dt_done, "dtu": dtu_done, "x": x_silued, "z": z_silued}

            def mamba_scan(unit):
                b, seg = divmod(unit, NSEG)
                s = unit % 2
                ready = front_ready[unit]
                rows = {}

                def fetch(n):
                    k = (unit * NS + n) % DEEP
                    src = a["scratch"][unit]
                    rows[n] = (load(sp, f"B{k}", [(Bn[k][:, :], src[n:n + 1, :].broadcast_to([P, SEG]))],
                                    ready["stored"], bn_free[k]),
                               load(sp, f"C{k}", [(Cn[k][:, :], src[NS + n:NS + n + 1, :].broadcast_to([P, SEG]))],
                                    cn_free[k]))

                for n in range(DEEP):
                    fetch(n)
                m = pe.do([mm(psum[Y_BANKS[j]][:, :], diag_d[:, j, :], xc[s][:, j, :], True, False, loose=True)
                           for j in range(DT)], ready["x"], d_ready, [bank_free[k] for k in Y_BANKS])
                made = {}

                def make(item):
                    n, j = divmod(item, DT)
                    nb, i = (unit * NS + n) % DEEP, item % AHEAD
                    m1 = act.do(fn(dA[i][:, :], dtv[s][:, j, :], ACT.Exp, scale=m_A[:, j, n:n + 1]), ready["dt"],
                                m_a_ready, da_free[i])
                    m2 = pool.do(tt(dBu[i][:, :], dtu[s][:, j, :], Bn[nb][:, :], MUL), ready["dtu"], rows[n][0],
                                 dbu_free[i])
                    bn_free[nb] = m2
                    made[item] = [m1, m2]

                pending = []
                out_steps = mamba_out(unit - 1) if unit else iter(())
                for item in range(LEAD):
                    make(item)
                for item in range(NS * DT):
                    n, j = divmod(item, DT)
                    nb, k, i = (unit * NS + n) % DEEP, item % DEEP, item % AHEAD
                    if item + LEAD < NS * DT:
                        make(item + LEAD)
                    start = 0.0 if seg == 0 else carry[:, item:item + 1]
                    m3 = dve.do(lambda e, k=k, i=i, start=start: e.tensor_tensor_scan(
                        hs[k][:, :], dA[i][:, :], dBu[i][:, :], start, MUL, ADD), made[item], hs_free[k],
                        carried[0] if seg else None)
                    da_free[i] = dbu_free[i] = m3
                    m4 = dve.do(tt(hc[i][:, :], hs[k][:, :], Cn[nb][:, :], MUL), m3, rows[n][1], hc_free[i])
                    hs_free[k] = cn_free[nb] = m4
                    pending.append((j, k, i, n, m4, slice(item, item + 1)))
                    if len(pending) > 1:
                        m5 = gather(seg, *pending.pop(0))
                    if j == DT - 1 and n + DEEP < NS:
                        fetch(n + DEEP)
                    if item >= 3:
                        next(out_steps, None)
                    yield
                m5 = gather(seg, *pending.pop(0))
                scan_done[unit] = [m3, m5]
                for j in range(DT):
                    bank = Y_BANKS[j]
                    gated_y[unit] = bank_free[bank] = dve.do(tt(y[:, j, :], psum[bank][:, :], zs[s][:, j, :], MUL), m5,
                                                             ready["z"], m_ready.get(unit - 1))
                yield

            carried = [None]

            def gather(seg, j, k, i, n, made, col):
                m = hc_free[i] = pe.do(mm(psum[Y_BANKS[j]][:, :], eye[:, :], hc[i][:, :], False, n == NS - 1,
                                          loose=True), made)
                if seg + 1 < NSEG:
                    carried[0] = act.do(fn(carry[:, col], hs[k][:, SEG - 1:SEG], ACT.Copy), made)
                    hs_free[k] = [made, carried[0]]
                return m

            def mamba_out(unit):
                xcols = slice(unit * SEG, (unit + 1) * SEG)
                made = []
                for k in range(KT):
                    bank = O_BANKS[k]
                    made.append(pe.do(
                        [mm(psum[bank][:, :], w_o[:, j, k * P:(k + 1) * P], y[:, j, :], j == 0, False)
                         for j in range(DT)] +
                        [mm(psum[bank][:, :], eye[:, :], mu[unit % 3][:, k, :], False, True)],
                        gated_y[unit], mu_ready[unit], bank_free[bank]))
                    for _ in range(4):
                        yield
                for k in range(KT):
                    bank = O_BANKS[k]
                    m_ready[unit] = bank_free[bank] = dve.do(tt(xT[:, k, xcols], xT[:, k, xcols], psum[bank][:, :],
                                                                ADD), made[k])
                    yield

            lengths = {}
            for stage in range(-1, UNITS):
                streams = []
                if 0 <= stage:
                    streams.append(("scan", mamba_scan(stage)))
                if stage + 1 < UNITS:
                    streams.append(("front", mamba_front(stage + 1)))
                braid(streams, lengths)
            for _ in mamba_out(UNITS - 1):
                pass

        fence()
        final = swiglu("1", m_ready)
        outs = None
        for n in range(NB * T // SEG):
            cols = slice(n * SEG, (n + 1) * SEG)
            outs = load(sp, "out", [(out[:, :, cols], xT[:, :, cols])], final[n])
        sp.wait(outs)

        block = ctx.enter_context(nc.Block())

        @block.tensor
        def _(eng):
            pe.play(eng)

        @block.vector
        def _(eng):
            dve.play(eng)

        @block.scalar
        def _(eng):
            act.play(eng)

        @block.gpsimd
        def _(eng):
            pool.play(eng)

        @block.sync
        def _(eng):
            sp.play(eng)


def kernel(**inputs):
    import numpy as np
    import concourse.bacc as bacc
    from concourse.bass_utils import run_bass_kernel_spmd

    i = {k: np.asarray(v) for k, v in inputs.items()}
    A, B, FN = "L0_attn_a_", "L0_attn_b_", "L0_ffn_"

    def rows(w):
        return w.reshape(-1, P, w.shape[1]).transpose(1, 0, 2)

    x = i[A + "hidden_states"]
    heads = np.concatenate(
        [rows(i[A + w]).reshape(P, KT, H, P).transpose(2, 0, 1, 3).reshape(H, P, KT * P) for w in ("Wq", "Wk", "Wv")] +
        [i[A + "Wfb"].reshape(P, H, P).transpose(1, 0, 2)], axis=2)
    out_w = np.concatenate([i[A + "Wgb"].reshape(P, H, P).transpose(1, 0, 2), i[A + "Wo"].reshape(H, P, HID)], axis=2)
    conv = np.stack([i[A + c].reshape(H, P, KC) for c in ("conv_q", "conv_k", "conv_v")], axis=1)
    j, col = np.arange(P)[:, None] % SUBB, np.arange(SUBB)[None, :]
    masks = [j == col] + [(j // (2 * h) == col // (2 * h)) & (j // h % 2 == 0) & (col // h % 2 == 1) for h in LEVELS]
    arrays = {
        "xT": rows(x.reshape(NB * T, HID).T),
        "eye": np.eye(P, dtype=np.float32),
        "masks": np.stack(masks, axis=1).astype(np.float32),
        "head_w": heads,
        "out_w": out_w,
        "wfa": rows(i[A + "Wfa"]), "wga": rows(i[A + "Wga"]), "wb": rows(i[A + "Wb"]),
        "taps": conv.transpose(2, 0, 1, 3),
        "dt_bias": i[A + "dt_bias"].reshape(H, P).T,
        "a_log": np.broadcast_to(i[A + "A_log"].reshape(1, H), (P, H)),
        "norm_w": i[A + "norm_w"].reshape(P, 1),
        "w_gate": rows(i[FN + "w_gate"].T), "w_up": rows(i[FN + "w_up"].T), "w_down": rows(i[FN + "w_down"].T),
        "w_in": rows(i[B + "in_proj_w"].T), "w_x": rows(i[B + "x_proj_w"].T), "w_o": rows(i[B + "out_proj_w"].T),
        "m_norm": i[B + "norm_w"].reshape(KT, P).T,
        "m_taps": i[B + "conv_w"].reshape(DT, P, KC).transpose(1, 0, 2),
        "m_cb": i[B + "conv_b"].reshape(DT, P).T,
        "m_dtw": i[B + "dt_w"].reshape(DT, P).T,
        "m_dtb": i[B + "dt_b"].reshape(DT, P).T,
        "m_D": i[B + "D_param"].reshape(DT, P).T,
        "m_A": i[B + "A_log"].reshape(DT, P, NS).transpose(1, 0, 2),
    }
    arrays = {k: np.ascontiguousarray(v) for k, v in arrays.items()}
    nc = bacc.Bacc("TRN2", target_bir_lowering=False, num_devices=1)
    aps = {k: nc.dram_tensor("in_" + k, v.shape, mybir.dt.from_np(v.dtype), kind="ExternalInput").ap()
           for k, v in arrays.items()}
    aps["scratch"] = nc.dram_tensor("ssm_rows", (NB * NSEG, NX, SEG), F32, kind="Internal").ap()
    out = nc.dram_tensor("out_xT", (P, KT, NB * T), F32, kind="ExternalOutput").ap()
    hybrid_block(nc, aps, out)
    r = run_bass_kernel_spmd(nc, [{"in_" + k: v for k, v in arrays.items()}], core_ids=[0])
    got = r.results[0]["out_xT"]
    return got.transpose(1, 0, 2).reshape(HID, NB, T).transpose(1, 2, 0)
```
